# Optimizing a Trainium2 kernel written in Bass

```python
import numpy as np
import jax
import jax.numpy as jnp

def _softmax(x, axis=-1):
    return jax.nn.softmax(x, axis=axis)

def _gelu(x):
    return jax.nn.gelu(x, approximate=True)

def _silu(x):
    return jax.nn.silu(x)

def _sigmoid(x):
    return jax.nn.sigmoid(x)

def _layernorm(x, axis=-1, eps=1e-05):
    m = jnp.mean(x, axis=axis, keepdims=True)
    v = jnp.var(x, axis=axis, keepdims=True)
    return (x - m) / jnp.sqrt(v + eps)

def _scatter_add(tgt, idx, src, axis=0):
    return tgt.at[idx].add(src)

def _segment_sum(src, seg, n):
    return jax.ops.segment_sum(src, seg, n)
kernel_name = 'mk_flamingo_gated_d1_seqx_r8_361fb1'

def setup_inputs(seed: int=0):
    np.random.seed(seed)
    _w = jnp.asarray

    def _rec_inputs():
        import jax
        import jax.numpy as jnp
        _rk = jax.random.key(seed)
        x = 7.22e-05 + 1 * jax.random.normal(jax.random.fold_in(_rk, 1), (8, 128, 512), jnp.float32)
        _lenS = 128 - jax.random.randint(jax.random.fold_in(_rk, 7), (8,), 0, max(1, 128 // 4) + 1, jnp.int32)
        _lenS2 = 128 - jax.random.randint(jax.random.fold_in(_rk, 8), (8,), 0, max(1, 128 // 4) + 1, jnp.int32)
        _ctx_4096P = jax.random.normal(jax.random.fold_in(_rk, 11), (8, 16, 512), jnp.float32)
        _ctx_4096c = jax.random.dirichlet(jax.random.fold_in(_rk, 511), 0.3 * jnp.ones((16,), jnp.float32), (8, 128))
        _ctx_4096t = jnp.einsum('bsk,bkd->bsd', _ctx_4096c, _ctx_4096P)
        _ctx_4096t = _ctx_4096t * jax.lax.rsqrt(jnp.mean(jnp.square(_ctx_4096t)) + 1e-12) * 0.953939
        ctx_4096 = 4.13588e-05 + 0.999923 * (_ctx_4096t + 0.3 * jax.random.normal(jax.random.fold_in(_rk, 611), (8, 128, 512), jnp.float32))
        _validS = jnp.arange(128)[None, :] < _lenS[:, None]
        _validS2 = jnp.arange(128)[None, :] < _lenS2[:, None]
        _causal = jnp.tril(jnp.ones((128, 128), dtype=bool))
        mask_BxSxS2_bk0 = jnp.logical_not(jnp.broadcast_to(_validS2[:, None, :], (8, 128, 128)))
        _g = jax.random.normal(jax.random.fold_in(_rk, 9001), (2, 1), jnp.float32)
        _g = jnp.sign(_g) * jnp.maximum(jnp.abs(_g), 1.0) + (_g == 0) * 1.0
        g_xattn = _g[0]
        g_ffn = _g[1]
        return (x, ctx_4096, mask_BxSxS2_bk0, g_xattn, g_ffn)
    x, ctx_4096, mask_BxSxS2_bk0, g_xattn, g_ffn = _rec_inputs()

    def _L0_xattn_setup():
        import jax, jax.numpy as jnp
        import numpy as np
        B, LQ, LK, D, H, DH = (2, 128, 128, 512, 32, 128)
        EPS = 1e-05

        def _rmsnorm(x, weight):
            var = jnp.mean(jnp.square(x), axis=-1, keepdims=True)
            return x * jax.lax.rsqrt(var + EPS) * weight
        key = jax.random.key(seed)
        ks = jax.random.split(key, 8)
        scale = 0.02
        return {'hidden_states': jax.random.normal(ks[0], (B, LQ, D), jnp.float32), 'key_value_states': jax.random.normal(ks[1], (B, LK, D), jnp.float32), 'attention_mask': jax.random.randint(ks[2], (B, LQ, LK), 0, 2) > 0, 'position_bias': jax.random.normal(ks[3], (H, LQ, LK), jnp.float32), 'ln_weight': jnp.ones((D,), jnp.float32), 'w_q': jax.random.normal(ks[4], (H * DH, D), jnp.float32) * scale, 'w_k': jax.random.normal(ks[5], (H * DH, D), jnp.float32) * scale, 'w_v': jax.random.normal(ks[6], (H * DH, D), jnp.float32) * scale, 'w_out': jax.random.normal(ks[7], (D, H * DH), jnp.float32) * scale}
    _L0_xattn_all = _L0_xattn_setup()
    _L0_xattn_in = {k: v for k, v in _L0_xattn_all.items() if k in ('position_bias', 'ln_weight', 'w_q', 'w_k', 'w_v', 'w_out')}
    del _L0_xattn_all

    def _L0_ffn_setup():
        import jax, jax.numpy as jnp
        import numpy as np
        R = 16
        NUM_EXPERTS = 8
        TOP_K = 2
        LORA_ALPHA = 32
        SCALING = LORA_ALPHA / R
        key = jax.random.key(seed)
        ks = jax.random.split(key, 6)
        d_in, d_out = (512, 512)
        x = jax.random.normal(ks[0], (4, 256, d_in), dtype=jnp.float32)
        W_base = jax.random.normal(ks[1], (d_out, d_in), dtype=jnp.float32) * 0.02
        b_base = jax.random.normal(ks[2], (d_out,), dtype=jnp.float32) * 0.02
        W_router = jax.random.normal(ks[3], (NUM_EXPERTS, d_in), dtype=jnp.float32) * 0.01
        A = jax.random.normal(ks[4], (NUM_EXPERTS, R, d_in), dtype=jnp.float32) * 0.02
        B = jax.random.normal(ks[5], (NUM_EXPERTS, d_out, R), dtype=jnp.float32) * 0.02
        return {'x': x, 'W_base': W_base, 'b_base': b_base, 'W_router': W_router, 'A': A, 'B': B}
    _L0_ffn_all = _L0_ffn_setup()
    _L0_ffn_in = {k: v for k, v in _L0_ffn_all.items() if k in ('W_base', 'b_base', 'W_router', 'A', 'B')}
    del _L0_ffn_all
    return {'x': x, 'ctx_4096': ctx_4096, 'mask_BxSxS2_bk0': mask_BxSxS2_bk0, 'g_xattn': g_xattn, 'g_ffn': g_ffn, 'L0_xattn_position_bias': _L0_xattn_in['position_bias'], 'L0_xattn_ln_weight': _L0_xattn_in['ln_weight'], 'L0_xattn_w_q': _L0_xattn_in['w_q'], 'L0_xattn_w_k': _L0_xattn_in['w_k'], 'L0_xattn_w_v': _L0_xattn_in['w_v'], 'L0_xattn_w_out': _L0_xattn_in['w_out'], 'L0_ffn_W_base': _L0_ffn_in['W_base'], 'L0_ffn_b_base': _L0_ffn_in['b_base'], 'L0_ffn_W_router': _L0_ffn_in['W_router'], 'L0_ffn_A': _L0_ffn_in['A'], 'L0_ffn_B': _L0_ffn_in['B']}

def reference(x, ctx_4096, mask_BxSxS2_bk0, g_xattn, g_ffn, L0_xattn_position_bias, L0_xattn_ln_weight, L0_xattn_w_q, L0_xattn_w_k, L0_xattn_w_v, L0_xattn_w_out, L0_ffn_W_base, L0_ffn_b_base, L0_ffn_W_router, L0_ffn_A, L0_ffn_B):
    import jax
    import jax.numpy as jnp

    def _L0_xattn_ref(hidden_states, key_value_states, attention_mask, position_bias, ln_weight, w_q, w_k, w_v, w_out):
        import jax, jax.numpy as jnp
        import numpy as np
        B, LQ, LK, D, H, DH = (2, 128, 128, 512, 32, 128)
        EPS = 1e-05

        def _rmsnorm(x, weight):
            var = jnp.mean(jnp.square(x), axis=-1, keepdims=True)
            return x * jax.lax.rsqrt(var + EPS) * weight
        x = _rmsnorm(hidden_states, ln_weight)
        b, lq, _ = x.shape
        lk = key_value_states.shape[1]
        h_q = (x @ w_q.T).reshape(b, lq, H, DH)
        h_k = (key_value_states @ w_k.T).reshape(b, lk, H, DH)
        h_v = (key_value_states @ w_v.T).reshape(b, lk, H, DH)
        score = jnp.einsum('bqhd,bkhd->bhqk', h_q, h_k)
        score = score + position_bias[None]
        m = attention_mask[:, None]
        score = jnp.where(m, score, -jnp.inf)
        score = jax.nn.softmax(score, axis=-1)
        score = jnp.where(m, score, 0.0)
        attn = jnp.einsum('bhqk,bkhd->bqhd', score, h_v).reshape(b, lq, H * DH)
        out = attn @ w_out.T
        return hidden_states + out

    def _L0_ffn_ref(x, W_base, b_base, W_router, A, B):
        import jax, jax.numpy as jnp
        import numpy as np
        R = 16
        NUM_EXPERTS = 8
        TOP_K = 2
        LORA_ALPHA = 32
        SCALING = LORA_ALPHA / R
        orig_shape = x.shape
        d_in = x.shape[-1]
        x_flat = x.reshape(-1, d_in)
        logits = x_flat @ W_router.T
        probs = jax.nn.softmax(logits, axis=-1)
        topk_probs, topk_idx = jax.lax.top_k(probs, TOP_K)
        topk_probs = topk_probs / jnp.sum(topk_probs, axis=-1, keepdims=True)
        onehot = jax.nn.one_hot(topk_idx, NUM_EXPERTS, dtype=x.dtype)
        combine = jnp.einsum('nk,nke->ne', topk_probs, onehot)
        h = jnp.einsum('nd,erd->ner', x_flat, A)
        hw = h * combine[:, :, None]
        expert_out = jnp.einsum('ner,eor->no', hw, B) * SCALING
        base_out = x_flat @ W_base.T + b_base
        out = base_out + expert_out
        return out.reshape(*orig_shape[:-1], W_base.shape[0])
    x = x + jnp.tanh(g_xattn[0]) * _L0_xattn_ref(_layernorm(x, axis=-1), ctx_4096, mask_BxSxS2_bk0, L0_xattn_position_bias, L0_xattn_ln_weight, L0_xattn_w_q, L0_xattn_w_k, L0_xattn_w_v, L0_xattn_w_out)
    x = x + jnp.tanh(g_ffn[0]) * _L0_ffn_ref(_layernorm(x, axis=-1), L0_ffn_W_base, L0_ffn_b_base, L0_ffn_W_router, L0_ffn_A, L0_ffn_B)
    return x

_drawn_inputs = setup_inputs


def setup_inputs(seed=0):
    import zlib

    import numpy as np

    out = dict(_drawn_inputs(seed))
    spreads = {'L0_xattn_ln_weight': (1.0, 0.538)}
    factors = {'L0_ffn_b_base': 5.633}
    for name, (base, spread) in spreads.items():
        noise = np.random.default_rng([zlib.crc32(name.encode()), seed]).standard_normal(out[name].shape)
        drawn = base * np.exp(spread * noise) if base else spread * noise
        out[name] = jnp.asarray(drawn.astype(out[name].dtype))
    for name, factor in factors.items():
        out[name] = (out[name] * factor).astype(out[name].dtype)
    return out
```

```python
from contextlib import ExitStack

import concourse.bass as bass
from concourse import mybir

F32 = mybir.dt.float32
F32R = mybir.dt.float32r
U8 = mybir.dt.uint8
U32 = mybir.dt.uint32
ALU = mybir.AluOpType
ACT = mybir.ActivationFunctionType
AX = mybir.AxisListType

P = 128
B = 8
D = 512
DC = D // P
H = 32
HALF = B // 2
W = HALF * P
PAIRS = H // 2
STEPS = 4 * PAIRS
E = 8
R = 16
ER = E * R
EPS = 1e-5
SCALING = 32 / R
MASKED = 1e30


def flamingo_block(nc, x, ctx_t, mask, gates, bias, ln_w, w_qk, w_v, w_o, w_base, w_lora, w_up, b_base, out):
    stack = ExitStack()
    with stack:
        def sb(name, shape, dt=F32):
            return stack.enter_context(nc.sbuf_tensor(name, shape, dt))

        def sem(name):
            return stack.enter_context(nc.semaphore(name))

        acc = sb("acc", [P, B, D])
        res = sb("res", [P, B, D])
        xt_hi = sb("xt_hi", [P, DC, B * P], F32R)
        xt_lo = sb("xt_lo", [P, DC, B * P], F32R)
        ct_hi = sb("ct_hi", [P, DC, B * P], F32R)
        ct_lo = sb("ct_lo", [P, DC, B * P], F32R)
        v_hi = sb("v_hi", [P, B, 2 * P], F32R)
        v_lo = sb("v_lo", [P, B, 2 * P], F32R)
        at_hi = sb("at_hi", [P, 4, W], F32R)
        at_lo = sb("at_lo", [P, 4, W], F32R)
        raw_qk = sb("raw_qk", [P, 2, 2 * D])
        raw_v = sb("raw_v", [P, 2 * D])
        raw_o = sb("raw_o", [P, 2 * D])
        wqk_hi = sb("wqk_hi", [P, 2, 2 * D], F32R)
        wqk_lo = sb("wqk_lo", [P, 2, 2 * D], F32R)
        wv_hi = sb("wv_hi", [P, DC, 2 * P], F32R)
        wv_lo = sb("wv_lo", [P, DC, 2 * P], F32R)
        wo_hi = sb("wo_hi", [P, 2, D], F32R)
        wo_lo = sb("wo_lo", [P, 2, D], F32R)
        q_hi = sb("q_hi", [P, W], F32R)
        q_lo = sb("q_lo", [P, W], F32R)
        k_hi = sb("k_hi", [P, W], F32R)
        k_lo = sb("k_lo", [P, W], F32R)
        sc = sb("sc", [P, W])
        pr = sb("pr", [P, W])
        pt_hi = sb("pt_hi", [P, W], F32R)
        pt_lo = sb("pt_lo", [P, W], F32R)
        bias_sb = sb("bias_sb", [P, 2, P])
        bm = sb("bm", [P, HALF, P])
        mask8 = sb("mask8", [P, B, P], U8)
        mneg = sb("mneg", [P, B, P])
        allowed = sb("allowed", [P, B])
        ident = sb("ident", [P, P])
        lnw = sb("lnw", [P, DC])
        gate = sb("gate", [P, 2])
        tg = sb("tg", [P, 2])
        half_pow = sb("half_pow", [P, HALF])
        stats = sb("stats", [P, B, 6])
        mv = sb("mv", [P, B, 2])
        var_e = sb("var_e", [P, B])
        rstd = sb("rstd", [P, B])
        rms = sb("rms", [P, B])
        nmax = sb("nmax", [P, HALF])
        sums = sb("sums", [P, HALF])
        rinv = sb("rinv", [P, HALF])
        expert = sb("expert", [P, E])
        lg = sb("lg", [P, HALF, E])
        lmax = sb("lmax", [P, HALF])
        lsum = sb("lsum", [P, HALF])
        linv = sb("linv", [P, HALF])
        top = sb("top", [P, HALF, 8])
        top_i = sb("top_i", [P, HALF, 8], U32)
        top_f = sb("top_f", [P, HALF, 2])
        tw = sb("tw", [P, HALF, 2])
        hot = sb("hot", [P, 2, HALF, E])
        comb = sb("comb", [P, HALF, E])
        bb = sb("bb", [P, D])

        ps_q, ps_k, ps_s, ps_t, ps_v, ps_a, ps_o0, ps_o1 = [
            stack.enter_context(nc.psum_tensor(f"ps_{n}", [P, W], F32))
            for n in ("q", "k", "s", "t", "v", "a", "o0", "o1")]
        ps_o = [ps_o0, ps_o1]
        ps_x = [[ps_s, ps_t, ps_o0, ps_o1],
                [ps_a, ps_t, ps_o0, ps_o1]]
        ps_x1 = [ps_t, ps_q, ps_s, ps_v, ps_t, ps_o1, ps_t, ps_o1]
        ps_lora = [ps_k, ps_q]
        ps_base = [ps_s, ps_v, ps_a, ps_o0]

        x_in = [sem("x_in0"), sem("x_in1")]
        ctx_in = [sem("ctx_in0"), sem("ctx_in1")]
        mask_in, small_in, bb_in = sem("mask_in"), sem("small_in"), sem("bb_in")
        wqk_in = [sem("wqk_in0"), sem("wqk_in1")]
        wv_in, wo_in, bias_in = sem("wv_in"), sem("wo_in"), sem("bias_in")
        res_in, ffn_in = sem("res_in"), sem("ffn_in")
        stored = sem("stored")
        ident_zero, ident_ok, consts_ok, pool_chain = sem("ident_zero"), sem("ident_ok"), sem("consts_ok"), sem("pool_chain")
        mneg_ok, allowed_ok, tanh_ok = sem("mneg_ok"), sem("allowed_ok"), sem("tanh_ok")
        bn_ok, mv_ok, scales_ok, xr_ok = sem("bn_ok"), sem("mv_ok"), sem("scales_ok"), sem("xr_ok")
        xr_used, xt_hi_ok, xt_lo_ok = sem("xr_used"), sem("xt_hi_ok"), sem("xt_lo_ok")
        ct_hi_ok, ct_lo_ok = sem("ct_hi_ok"), sem("ct_lo_ok")
        wqk_hi_ok = [sem("wqk_hi_ok0"), sem("wqk_hi_ok1")]
        wqk_lo_ok = [sem("wqk_lo_ok0"), sem("wqk_lo_ok1")]
        wv_hi_ok, wv_lo_ok, wo_hi_ok, wo_lo_ok = sem("wv_hi_ok"), sem("wv_lo_ok"), sem("wo_hi_ok"), sem("wo_lo_ok")
        q_ps, k_ps, s_ps, t_ps, v_ps, a_ps, o_ps = [sem(n) for n in ("q_ps", "k_ps", "s_ps", "t_ps", "v_ps", "a_ps", "o_ps")]
        q_hi_ok, q_lo_ok, k_hi_ok, k_lo_ok = [sem(n) for n in ("q_hi_ok", "q_lo_ok", "k_hi_ok", "k_lo_ok")]
        pt_hi_ok, pt_lo_ok, v_hi_ok, v_lo_ok = [sem(n) for n in ("pt_hi_ok", "pt_lo_ok", "v_hi_ok", "v_lo_ok")]
        at_hi_ok, at_lo_ok = sem("at_hi_ok"), sem("at_lo_ok")
        bm_ok, biased, nmax_ok, exp_ok, inv_ok, pr_ok, acc_ok = [
            sem(n) for n in ("bm_ok", "biased", "nmax_ok", "exp_ok", "inv_ok", "pr_ok", "acc_ok")]
        x1_ok, bn1_ok, mv1_ok, rstd1_ok, x1n_ok = [sem(n) for n in ("x1_ok", "bn1_ok", "mv1_ok", "rstd1_ok", "x1n_ok")]
        x1t_ps, x1t_hi_ok, x1t_lo_ok = sem("x1t_ps"), sem("x1t_hi_ok"), sem("x1t_lo_ok")
        bg_ok, x1b_ok = sem("bg_ok"), sem("x1b_ok")
        ffn_hi_ok, ffn_lo_ok = sem("ffn_hi_ok"), sem("ffn_lo_ok")
        lora_ps, base_ps, route, lexp_ok, hw_ok = [sem(n) for n in ("lora_ps", "base_ps", "route", "lexp_ok", "hw_ok")]
        hwt_ps, hwt_hi_ok, hwt_lo_ok, y_ps, y_ok = [sem(n) for n in ("hwt_ps", "hwt_hi_ok", "hwt_lo_ok", "y_ps", "y_ok")]

        ctx_raw = res[:, :, :].rearrange("p b d -> p (b d)").rearrange("p (h c n) -> p h c n", h=2, c=DC)
        xr_buf = [sc, pr]
        base_hi = wqk_hi[:, :, :].rearrange("p h n -> p (h n)").rearrange("p (c n) -> p c n", c=DC)
        base_lo = wqk_lo[:, :, :].rearrange("p h n -> p (h n)").rearrange("p (c n) -> p c n", c=DC)
        LW = ER + E
        lora_hi = wv_hi[:, :, :].rearrange("p c n -> p (c n)")[:, 0:DC * LW].rearrange("p (c n) -> p c n", c=DC)
        lora_lo = wv_lo[:, :, :].rearrange("p c n -> p (c n)")[:, 0:DC * LW].rearrange("p (c n) -> p c n", c=DC)
        up_hi, up_lo = q_hi, q_lo
        hw = bm[:, :, :]

        ROUTE_SHIFTED = 4
        ROUTE_STEPS = 24

        def wqk(w, hp, which, c):
            at = (which * DC + c) * P
            return w[:, hp, at:at + P]

        def three_passes(pe, dst, pairs, first=True, last=True):
            n, total = 0, 3 * len(pairs)
            for (l_hi, l_lo), (r_hi, r_lo) in pairs:
                for a, b in ((l_hi, r_hi), (l_hi, r_lo), (l_lo, r_hi)):
                    mm = pe.matmul(dst, a, b, start=first and n == 0, stop=last and n == total - 1)
                    n += 1
            return mm

        def batches(i):
            return (2 * i, 2 * i + 1)

        block = stack.enter_context(nc.Block())

        @block.sync
        def _(sp):
            sp.dma_start(acc[:, 0:HALF, :], x[:, 0:HALF, :]).then_inc(x_in[0], 16)
            sp.dma_start(raw_v[:, :], w_v[0, :, :]).then_inc(wv_in, 16)
            sp.dma_start(raw_qk[:, 0, :], w_qk[0, :, :]).then_inc(wqk_in[0], 16)
            sp.dma_start(acc[:, HALF:B, :], x[:, HALF:B, :]).then_inc(x_in[1], 16)
            sp.dma_start(raw_qk[:, 1, :], w_qk[1, :, :]).then_inc(wqk_in[1], 16)
            sp.dma_start(bias_sb[:, :, :], bias[0, :, :, :]).then_inc(bias_in, 16)
            sp.dma_start(raw_o[:, :], w_o[0, :, :]).then_inc(wo_in, 16)
            sp.dma_start(bb[:, :], b_base).then_inc(bb_in, 16)
            with sp.Fori(0, PAIRS - 1) as i:
                sp.wait_ge(wv_lo_ok, i + 1)
                sp.dma_start(raw_v[:, :], w_v[i + 1, :, :]).then_inc(wv_in, 16)
                for hp in range(2):
                    sp.wait_ge(wqk_lo_ok[hp], i + 1)
                    sp.dma_start(raw_qk[:, hp, :], w_qk[2 * i + (2 + hp), :, :]).then_inc(wqk_in[hp], 16)
                sp.wait_ge(wo_lo_ok, i + 1)
                sp.dma_start(raw_o[:, :], w_o[i + 1, :, :]).then_inc(wo_in, 16)
                sp.wait_ge(bm_ok, 4 * i + 4)
                sp.dma_start(bias_sb[:, :, :], bias[i + 1, :, :, :]).then_inc(bias_in, 16)
            sp.wait_ge(ct_lo_ok, 2)
            sp.dma_start(res[:, :, :], x).then_inc(res_in, 16)
            sp.wait_ge(wqk_lo_ok[0], PAIRS)
            sp.wait_ge(wqk_lo_ok[1], PAIRS)
            sp.dma_start(raw_qk[:, :, :].rearrange("p h n -> p (h n)"), w_base).then_inc(ffn_in, 16)
            sp.wait_ge(wv_lo_ok, PAIRS)
            sp.dma_start(raw_v[:, 0:DC * LW], w_lora).then_inc(ffn_in, 16)
            sp.wait_ge(wo_lo_ok, PAIRS)
            sp.dma_start(raw_o[:, 0:D], w_up).then_inc(ffn_in, 16)
            for t in range(B):
                sp.wait_ge(y_ok, t + 1)
                sp.dma_start(out[:, t, :], acc[:, t, :]).then_inc(stored, 16)
            sp.wait_ge(stored, 16 * B)

        @block.gpsimd
        def _(pool):
            pool.memset(ident[:, :], 0.0).then_inc(ident_zero, 1)
            pool.wait_ge(ident_zero, 1)
            pool.affine_select(out=ident[:, :], in_=ident[:, :], compare_op=ALU.not_equal, fill=1.0,
                               base=0, pattern=[[-1, P]], channel_multiplier=1).then_inc(ident_ok, 1)
            for e in range(E):
                pool.memset(expert[:, e:e + 1], float(e)).then_inc(consts_ok, 1)
            pool.memset(half_pow[:, :], -0.5).then_inc(consts_ok, 1)
            pool.wait_ge(consts_ok, E + 1)
            steps = [0]

            def link(op):
                op.then_inc(pool_chain, 1)
                steps[0] += 1
                pool.wait_ge(pool_chain, steps[0])

            def rsqrt(dst, src):
                link(pool.tensor_scalar(src, src, EPS, 0.0, ALU.add, ALU.add))
                return pool.tensor_tensor(dst, src, half_pow[:, :], ALU.pow)

            for h in range(2):
                own = slice(HALF * h, HALF * h + HALF)
                pool.wait_ge(mv_ok, HALF * h + HALF)
                link(pool.tensor_copy(var_e[:, own], mv[:, own, 1]))
                link(rsqrt(rstd[:, own], var_e[:, own]))
                link(pool.tensor_tensor(rms[:, own], rstd[:, own], rstd[:, own], ALU.mult))
                link(pool.tensor_tensor(rms[:, own], rms[:, own], mv[:, own, 1], ALU.mult))
                link(pool.tensor_scalar(rms[:, own], rms[:, own], EPS, 0.0, ALU.add, ALU.add))
                pool.tensor_tensor(rms[:, own], rms[:, own], half_pow[:, :], ALU.pow).then_inc(scales_ok, 1)
                if h == 0:
                    pool.wait_ge(mask_in, 16)
                    pool.tensor_scalar(mneg[:, :, :], mask8[:, :, :], -1.0, MASKED, ALU.add, ALU.mult).then_inc(mneg_ok, 1)
                    pool.wait_ge(mneg_ok, 1)

            def mask_step(s, j, g):
                if j == 0:
                    pool.wait_ge(bias_in, 16 * g + 16)
                own = slice(HALF * (j // 2), HALF * (j // 2) + HALF)
                head_bias = bias_sb[:, j % 2:j % 2 + 1, :].to_broadcast([P, HALF, P])
                pool.tensor_tensor(bm[:, :, :], head_bias, mneg[:, own, :], ALU.add).then_inc(bm_ok, 1)

            mask_step(0, 0, 0)
            pool.wait_ge(biased, 1)
            mask_step(1, 1, 0)
            with pool.Fori(0, PAIRS - 1) as i:
                for n, (j, g) in enumerate(((2, i), (3, i), (0, i + 1), (1, i + 1))):
                    s = 4 * i + (2 + n)
                    pool.wait_ge(biased, s)
                    mask_step(s, j, g)
            for s in range(STEPS - 2, STEPS):
                pool.wait_ge(biased, s)
                mask_step(s, s % 4, PAIRS - 1)

            for h in range(2):
                own = slice(HALF * h, HALF * h + HALF)
                pool.wait_ge(mv1_ok, HALF * h + HALF)
                link(pool.tensor_copy(var_e[:, own], mv[:, own, 1]))
                rsqrt(rstd[:, own], var_e[:, own]).then_inc(rstd1_ok, 1)
                if h == 0:
                    pool.wait_ge(bg_ok, 1)
                pool.wait_ge(x1n_ok, HALF * h + HALF)
                for t in range(HALF * h, HALF * h + HALF):
                    pool.tensor_tensor(res[:, t, :], res[:, t, :], bb[:, :], ALU.add).then_inc(x1b_ok, 1)

        @block.scalar
        def _(act):
            act.dma_start(ctx_raw[:, 0, :, :], ctx_t[0, :, :, :]).then_inc(ctx_in[0], 16)
            act.dma_start(lnw[:, :], ln_w).then_inc(small_in, 16)
            act.dma_start(gate[:, :], gates).then_inc(small_in, 16)
            act.dma_start(ctx_raw[:, 1, :, :], ctx_t[1, :, :, :]).then_inc(ctx_in[1], 16)
            act.dma_start(mask8[:, :, :], mask).then_inc(mask_in, 16)

            def ctx_part(h):
                act.wait_ge(ctx_in[h], 16)
                act.activation(ct_hi[:, :, W * h:W * h + W], ctx_raw[:, h, :, :], ACT.Copy).then_inc(ct_hi_ok, 1)

            def split_wqk(hp, g):
                act.wait_ge(wqk_in[hp], 16 * g + 16)
                act.activation(wqk_hi[:, hp, :], raw_qk[:, hp, :], ACT.Copy).then_inc(wqk_hi_ok[hp], 1)

            def split_wv(g):
                act.wait_ge(wv_in, 16 * g + 16)
                act.activation(wv_hi[:, :, :], raw_v[:, :], ACT.Copy).then_inc(wv_hi_ok, 1)

            def split_wo(g):
                act.wait_ge(wo_in, 16 * g + 16)
                act.activation(wo_hi[:, :, :], raw_o[:, :], ACT.Copy).then_inc(wo_hi_ok, 1)

            def split_q(s):
                act.wait_ge(q_ps, s + 1)
                act.activation(q_hi[:, :], ps_q[:, :], ACT.Copy).then_inc(q_hi_ok, 1)

            def split_k(s):
                act.wait_ge(k_ps, s + 1)
                act.activation(k_hi[:, :], ps_k[:, :], ACT.Copy).then_inc(k_hi_ok, 1)

            def split_v(u, i):
                act.wait_ge(v_ps, u + 1)
                act.activation(v_hi[:, 2 * i:2 * i + 2, :], ps_v[:, :], ACT.Copy).then_inc(v_hi_ok, 1)

            def scale_tokens(h):
                act.wait_ge(scales_ok, h + 1)
                for t in range(HALF * h, HALF * h + HALF):
                    act.wait_ge(acc_ok, t + 1)
                    if t >= 2:
                        act.wait_ge(xr_used, t - 1)
                    act.activation(xr_buf[t % 2][:, :], acc[:, t, :], ACT.Copy, scale=rms[:, t:t + 1]).then_inc(xr_ok, 1)

            def token_hi(h):
                act.wait_ge(xr_used, HALF * h + HALF)
                for c in range(DC):
                    act.activation(xt_hi[:, c, W * h:W * h + W], ps_x[h][c][:, :], ACT.Copy,
                                   scale=lnw[:, c:c + 1]).then_inc(xt_hi_ok, 1)

            ctx_part(0)
            split_wv(0)
            split_wqk(0, 0)
            split_v(0, 0)
            split_v(1, 1)
            split_k(0)
            act.wait_ge(small_in, 32)
            scale_tokens(0)
            token_hi(0)
            split_q(0)
            act.activation(tg[:, :], gate[:, :], ACT.Tanh).then_inc(tanh_ok, 1)
            ctx_part(1)
            split_wqk(1, 0)
            scale_tokens(1)
            token_hi(1)

            def slot(s, j, g, qk=True, v=True):
                if j == 2 and v:
                    act.wait_ge(v_ps, s + 2)
                    split_wv(g + 1)
                act.wait_ge(nmax_ok, s + 1)
                for k in range(HALF):
                    own = slice(P * k, P * k + P)
                    last = act.activation(pr[:, own], sc[:, own], ACT.Exp, bias=nmax[:, k:k + 1], accum_out=sums[:, k:k + 1])
                last.then_inc(exp_ok, 1)
                if qk:
                    split_q(s + 1)
                if j == 2:
                    split_wo(g)
                if qk:
                    split_k(s + 1)
                act.wait_ge(t_ps, s + 1)
                act.activation(pt_hi[:, :], ps_t[:, :], ACT.Copy).then_inc(pt_hi_ok, 1)
                if j >= 2 and v:
                    split_wqk(j - 2, g + 1)
                if v:
                    split_v(s + 2, (j + 2) % 4)
                act.wait_ge(a_ps, s + 1)
                act.activation(at_hi[:, j, :], ps_a[:, :], ACT.Copy).then_inc(at_hi_ok, 1)

            slot(0, 0, 0)
            slot(1, 1, 0)
            with act.Fori(0, PAIRS - 1) as i:
                slot(4 * i + 2, 2, i)
                slot(4 * i + 3, 3, i)
                slot(4 * i + 4, 0, i + 1)
                slot(4 * i + 5, 1, i + 1)
            slot(STEPS - 2, 2, PAIRS - 1, v=False)
            act.wait_ge(ffn_in, 48)
            act.activation(lora_hi, raw_v[:, 0:DC * LW], ACT.Copy).then_inc(ffn_hi_ok, 1)
            slot(STEPS - 1, 3, PAIRS - 1, qk=False, v=False)
            act.activation(base_hi, raw_qk[:, :, :].rearrange("p h n -> p (h n)"), ACT.Copy).then_inc(ffn_hi_ok, 1)
            act.activation(up_hi[:, :], raw_o[:, 0:D], ACT.Copy).then_inc(ffn_hi_ok, 1)

            def x1_hi(h):
                for t in range(HALF * h, HALF * h + HALF):
                    act.wait_ge(x1t_ps, t + 1)
                    act.activation(xt_hi[:, :, P * t:P * t + P], ps_x1[t][:, :], ACT.Copy).then_inc(x1t_hi_ok, 1)

            def router_exp(h):
                act.wait_ge(route, ROUTE_STEPS * h + ROUTE_SHIFTED)
                act.activation(lg[:, :, :], lg[:, :, :], ACT.Exp).then_inc(lexp_ok, 1)

            def hwt_hi(h):
                act.wait_ge(hwt_ps, h + 1)
                act.activation(pt_hi[:, :], ps_t[:, :], ACT.Copy).then_inc(hwt_hi_ok, 1)

            x1_hi(0)
            router_exp(0)
            x1_hi(1)
            hwt_hi(0)
            router_exp(1)
            hwt_hi(1)

        @block.vector
        def _(ve):
            def lo(dst, src, hi):
                return ve.tensor_tensor(dst, src, hi.bitcast(F32), ALU.subtract)

            def moments(h, src, bn_sem, mv_sem, before=None):
                for t in range(HALF * h, HALF * h + HALF):
                    if before:
                        before(t)
                    ve.bn_stats(stats[:, t, :], src[:, t, :]).then_inc(bn_sem, 1)
                    ve.wait_ge(bn_sem, t + 1)
                    ve.bn_aggr(mv[:, t, :], stats[:, t, :]).then_inc(mv_sem, 1)

            def center(h):
                ve.wait_ge(mv_ok, HALF * h + HALF)
                ve.wait_ge(scales_ok, h + 1)
                for t in range(HALF * h, HALF * h + HALF):
                    ve.tensor_scalar(acc[:, t, :], acc[:, t, :], mv[:, t, 0:1], rstd[:, t:t + 1],
                                     ALU.subtract, ALU.mult).then_inc(acc_ok, 1)

            def ctx_part(h):
                ve.wait_ge(ct_hi_ok, h + 1)
                lo(ct_lo[:, :, W * h:W * h + W], ctx_raw[:, h, :, :], ct_hi[:, :, W * h:W * h + W]).then_inc(ct_lo_ok, 1)

            def split_wqk(hp, g):
                ve.wait_ge(wqk_hi_ok[hp], g + 1)
                lo(wqk_lo[:, hp, :], raw_qk[:, hp, :], wqk_hi[:, hp, :]).then_inc(wqk_lo_ok[hp], 1)

            def split_wv(g):
                ve.wait_ge(wv_hi_ok, g + 1)
                lo(wv_lo[:, :, :], raw_v[:, :].rearrange("p (c n) -> p c n", c=DC), wv_hi[:, :, :]).then_inc(wv_lo_ok, 1)

            def split_wo(g):
                ve.wait_ge(wo_hi_ok, g + 1)
                lo(wo_lo[:, :, :], raw_o[:, :].rearrange("p (c n) -> p c n", c=2), wo_hi[:, :, :]).then_inc(wo_lo_ok, 1)

            def split_q(s):
                ve.wait_ge(q_hi_ok, s + 1)
                lo(q_lo[:, :], ps_q[:, :], q_hi[:, :]).then_inc(q_lo_ok, 1)

            def split_k(s):
                ve.wait_ge(k_hi_ok, s + 1)
                lo(k_lo[:, :], ps_k[:, :], k_hi[:, :]).then_inc(k_lo_ok, 1)

            def split_v(u, i):
                ve.wait_ge(v_hi_ok, u + 1)
                own = slice(2 * i, 2 * i + 2)
                lo(v_lo[:, own, :], ps_v[:, :].rearrange("p (b n) -> p b n", b=2), v_hi[:, own, :]).then_inc(v_lo_ok, 1)

            def token_lo(h):
                for c in range(DC):
                    ve.wait_ge(xt_hi_ok, DC * h + c + 1)
                    own = slice(W * h, W * h + W)
                    ve.scalar_tensor_tensor(xt_lo[:, c, own], ps_x[h][c][:, :], lnw[:, c:c + 1],
                                            xt_hi[:, c, own].bitcast(F32), ALU.mult, ALU.subtract).then_inc(xt_lo_ok, 1)

            def accumulate(w, i):
                for n, t in enumerate(batches(i)):
                    ve.wait_ge(o_ps, 2 * w + (n + 1))
                    ve.tensor_tensor(acc[:, t, :], ps_o[n][:, :], acc[:, t, :], ALU.add).then_inc(acc_ok, 1)

            ve.wait_ge(x_in[0], 16)
            moments(0, acc, bn_ok, mv_ok)
            ctx_part(0)
            split_wv(0)
            center(0)
            split_wqk(0, 0)
            split_v(0, 0)
            split_v(1, 1)
            split_k(0)
            ve.wait_ge(small_in, 32)
            token_lo(0)
            split_q(0)
            ve.wait_ge(x_in[1], 16)
            moments(1, acc, bn_ok, mv_ok)
            ctx_part(1)
            split_wqk(1, 0)
            center(1)
            ve.wait_ge(mask_in, 16)
            ve.tensor_reduce(allowed[:, :], mask8[:, :, :], AX.X, ALU.max).then_inc(allowed_ok, 1)
            ve.wait_ge(allowed_ok, 1)
            token_lo(1)

            def slot(s, j, g, qk=True, v=True, o=True):
                ve.wait_ge(s_ps, s + 1)
                ve.wait_ge(bm_ok, s + 1)
                ve.tensor_tensor(sc[:, :], ps_s[:, :], bm[:, :, :].rearrange("p b k -> p (b k)"), ALU.add).then_inc(biased, 1)
                ve.wait_ge(biased, s + 1)
                ve.tensor_reduce(nmax[:, :], sc[:, :].rearrange("p (b k) -> p b k", b=HALF), AX.X, ALU.max,
                                 negate=True).then_inc(nmax_ok, 1)
                if j == 2 and v:
                    split_wv(g + 1)
                ve.wait_ge(exp_ok, s + 1)
                ve.reciprocal(rinv[:, :], sums[:, :]).then_inc(inv_ok, 1)
                ve.wait_ge(inv_ok, s + 1)
                for k in range(HALF):
                    own = slice(P * k, P * k + P)
                    t = HALF * (j // 2) + k
                    last = ve.tensor_scalar(pr[:, own], pr[:, own], rinv[:, k:k + 1], allowed[:, t:t + 1],
                                            ALU.mult, ALU.mult)
                last.then_inc(pr_ok, 1)
                if qk:
                    split_q(s + 1)
                if j == 2:
                    split_wo(g)
                if qk:
                    split_k(s + 1)
                ve.wait_ge(pt_hi_ok, s + 1)
                lo(pt_lo[:, :], ps_t[:, :], pt_hi[:, :]).then_inc(pt_lo_ok, 1)
                if j >= 2 and v:
                    split_wqk(j - 2, g + 1)
                if v:
                    split_v(s + 2, (j + 2) % 4)
                ve.wait_ge(at_hi_ok, s + 1)
                lo(at_lo[:, j, :], ps_a[:, :], at_hi[:, j, :]).then_inc(at_lo_ok, 1)
                if o:
                    accumulate(s - 2, (j + 2) % 4)

            slot(0, 0, 0, o=False)
            slot(1, 1, 0, o=False)
            with ve.Fori(0, PAIRS - 1) as i:
                slot(4 * i + 2, 2, i)
                slot(4 * i + 3, 3, i)
                slot(4 * i + 4, 0, i + 1)
                slot(4 * i + 5, 1, i + 1)
            slot(STEPS - 2, 2, PAIRS - 1, v=False)
            ve.wait_ge(ffn_hi_ok, 1)
            lo(lora_lo, raw_v[:, 0:DC * LW].rearrange("p (c n) -> p c n", c=DC), lora_hi).then_inc(ffn_lo_ok, 1)
            slot(STEPS - 1, 3, PAIRS - 1, qk=False, v=False)

            def residual(h):
                def add(t):
                    ve.scalar_tensor_tensor(res[:, t, :], acc[:, t, :], tg[:, 0:1], res[:, t, :],
                                            ALU.mult, ALU.add).then_inc(x1_ok, 1)
                    ve.wait_ge(x1_ok, t + 1)
                moments(h, res, bn1_ok, mv1_ok, add)

            def center1(h):
                ve.wait_ge(rstd1_ok, h + 1)
                for t in range(HALF * h, HALF * h + HALF):
                    ve.tensor_scalar(acc[:, t, :], res[:, t, :], mv[:, t, 0:1], rstd[:, t:t + 1],
                                     ALU.subtract, ALU.mult).then_inc(x1n_ok, 1)

            def x1_lo(h):
                for t in range(HALF * h, HALF * h + HALF):
                    ve.wait_ge(x1t_hi_ok, t + 1)
                    own = slice(P * t, P * t + P)
                    lo(xt_lo[:, :, own], ps_x1[t][:, :].rearrange("p (c n) -> p c n", c=DC),
                       xt_hi[:, :, own]).then_inc(x1t_lo_ok, 1)

            steps = [0]

            def link(op, wait=True):
                op.then_inc(route, 1)
                steps[0] += 1
                if wait:
                    ve.wait_ge(route, steps[0])

            def spread(ap, n):
                return ap.unsqueeze(2).to_broadcast([P, HALF, n])

            def routing(h):
                for n in range(2):
                    ve.wait_ge(lora_ps, 2 * h + n + 1)
                    logits = ps_lora[n][:, 0:2 * LW].rearrange("p (b n) -> p b n", b=2)[:, :, ER:LW]
                    link(ve.tensor_copy(lg[:, 2 * n:2 * n + 2, :], logits), wait=n == 1)
                link(ve.tensor_reduce(lmax[:, :], lg[:, :, :], AX.X, ALU.max))
                link(ve.tensor_tensor(lg[:, :, :], lg[:, :, :], spread(lmax[:, :], E), ALU.subtract))
                assert steps[0] == ROUTE_STEPS * h + ROUTE_SHIFTED
                ve.wait_ge(lexp_ok, h + 1)
                link(ve.tensor_reduce(lsum[:, :], lg[:, :, :], AX.X, ALU.add))
                link(ve.reciprocal(linv[:, :], lsum[:, :]))
                link(ve.tensor_tensor(lg[:, :, :], lg[:, :, :], spread(linv[:, :], E), ALU.mult))
                for k in range(HALF):
                    link(ve.max(top[:, k, :], lg[:, k, :]), wait=k == HALF - 1)
                for k in range(HALF):
                    link(ve.max_index(top_i[:, k, :], top[:, k, :], lg[:, k, :]), wait=k == HALF - 1)
                link(ve.tensor_copy(top_f[:, :, :], top_i[:, :, 0:2]), wait=False)
                link(ve.tensor_tensor(lsum[:, :], top[:, :, 0], top[:, :, 1], ALU.add))
                link(ve.reciprocal(linv[:, :], lsum[:, :]))
                link(ve.scalar_tensor_tensor(tw[:, :, :], top[:, :, 0:2], SCALING, spread(linv[:, :], 2), ALU.mult, ALU.mult))
                numbers = expert[:, :].unsqueeze(1).to_broadcast([P, HALF, E])
                for n in range(2):
                    link(ve.tensor_tensor(hot[:, n, :, :], numbers, spread(top_f[:, :, n], E), ALU.is_equal), wait=n == 1)
                for n in range(2):
                    link(ve.tensor_tensor(hot[:, n, :, :], hot[:, n, :, :], spread(tw[:, :, n], E), ALU.mult), wait=n == 1)
                link(ve.tensor_tensor(comb[:, :, :], hot[:, 0, :, :], hot[:, 1, :, :], ALU.add))
                assert steps[0] == ROUTE_STEPS * (h + 1)
                if h == 1:
                    ve.wait_ge(hwt_ps, 1)
                for n in range(2):
                    hidden = ps_lora[n][:, 0:2 * LW].rearrange("p (b n) -> p b n", b=2)[:, :, 0:ER]
                    weight = comb[:, 2 * n:2 * n + 2, :].unsqueeze(3).to_broadcast([P, 2, E, R])
                    ve.tensor_tensor(hw[:, 2 * n:2 * n + 2, :].rearrange("p b (e r) -> p b e r", e=E),
                                     hidden.rearrange("p b (e r) -> p b e r", e=E), weight, ALU.mult).then_inc(hw_ok, 1)

            def hwt_lo(h):
                ve.wait_ge(hwt_hi_ok, h + 1)
                lo(pt_lo[:, :], ps_t[:, :], pt_hi[:, :]).then_inc(hwt_lo_ok, 1)

            def finish(h):
                for t in range(HALF * h, HALF * h + HALF):
                    ve.wait_ge(y_ps, t + 1)
                    ve.wait_ge(x1b_ok, t + 1)
                    ve.scalar_tensor_tensor(acc[:, t, :], ps_base[t % 4][:, :], tg[:, 1:2], res[:, t, :],
                                            ALU.mult, ALU.add).then_inc(y_ok, 1)

            ve.wait_ge(tanh_ok, 1)
            ve.wait_ge(res_in, 16)
            residual(0)
            accumulate(STEPS - 2, 2)
            ve.wait_ge(bb_in, 16)
            ve.tensor_scalar(bb[:, :], bb[:, :], tg[:, 1:2], None, ALU.mult).then_inc(bg_ok, 1)
            center1(0)
            accumulate(STEPS - 1, 3)
            ve.wait_ge(ffn_hi_ok, 3)
            lo(base_lo, raw_qk[:, :, :].rearrange("p h n -> p (h n)").rearrange("p (c n) -> p c n", c=DC), base_hi).then_inc(ffn_lo_ok, 1)
            lo(up_lo[:, :], raw_o[:, 0:D], up_hi[:, :]).then_inc(ffn_lo_ok, 1)
            x1_lo(0)
            residual(1)
            routing(0)
            center1(1)
            x1_lo(1)
            hwt_lo(0)
            finish(0)
            routing(1)
            hwt_lo(1)
            finish(1)

        @block.tensor
        def _(pe):
            def project(dst, hp, which, token_hi, token_lo, half):
                own = slice(W * half, W * half + W)
                return three_passes(pe, dst, [((wqk(wqk_hi, hp, which, c), wqk(wqk_lo, hp, which, c)),
                                               (token_hi[:, c, own], token_lo[:, c, own])) for c in range(DC)])

            def queries(j):
                project(ps_q[:, :], j % 2, 0, xt_hi, xt_lo, j // 2).then_inc(q_ps, 1)

            def keys(j):
                project(ps_k[:, :], j % 2, 1, ct_hi, ct_lo, j // 2).then_inc(k_ps, 1)

            def values(i):
                for n, t in enumerate(batches(i)):
                    own = slice(P * t, P * t + P)
                    last = three_passes(pe, ps_v[:, 2 * P * n:2 * P * n + 2 * P],
                                        [((ct_hi[:, c, own], ct_lo[:, c, own]), (wv_hi[:, c, :], wv_lo[:, c, :]))
                                         for c in range(DC)])
                last.then_inc(v_ps, 1)

            def output(i):
                for n, t in enumerate(batches(i)):
                    own = slice(P * (t % HALF), P * (t % HALF) + P)
                    first = 2 * (t // HALF)
                    three_passes(pe, ps_o[n][:, :],
                                 [((at_hi[:, first + hp, own], at_lo[:, first + hp, own]),
                                   (wo_hi[:, hp, :], wo_lo[:, hp, :])) for hp in range(2)]).then_inc(o_ps, 1)

            def first_transposes(h):
                for t in range(HALF * h, HALF * h + HALF):
                    pe.wait_ge(xr_ok, t + 1)
                    for c in range(DC):
                        last = pe.transpose(ps_x[h][c][:, P * (t % HALF):P * (t % HALF) + P],
                                            xr_buf[t % 2][:, P * c:P * c + P], ident[:, :])
                    last.then_inc(xr_used, 1)

            pe.wait_ge(ct_lo_ok, 1)
            pe.wait_ge(wv_lo_ok, 1)
            values(0)
            pe.wait_ge(v_lo_ok, 1)
            values(1)
            pe.wait_ge(wqk_lo_ok[0], 1)
            keys(0)
            pe.wait_ge(ident_ok, 1)
            first_transposes(0)
            pe.wait_ge(xt_lo_ok, DC)
            queries(0)
            first_transposes(1)

            def slot(s, j, g, qk=True, v=True, o=True, start=False):
                nxt, ahead = (j + 1) % 4, (j + 2) % 4
                pe.wait_ge(q_lo_ok, s + 1)
                pe.wait_ge(k_lo_ok, s + 1)
                for k in range(HALF):
                    own = slice(P * k, P * k + P)
                    last = three_passes(pe, ps_s[:, own], [((q_hi[:, own], q_lo[:, own]), (k_hi[:, own], k_lo[:, own]))])
                last.then_inc(s_ps, 1)
                if qk:
                    if nxt < 2:
                        pe.wait_ge(wqk_lo_ok[nxt], (g + 1 if j == 3 else g) + 1)
                    if start and j == 1:
                        pe.wait_ge(ct_lo_ok, 2)
                        pe.wait_ge(xt_lo_ok, 2 * DC)
                    queries(nxt)
                    keys(nxt)
                if start and j == 0:
                    pe.wait_ge(xt_lo_ok, 2 * DC)
                    pe.wait_ge(ct_lo_ok, 2)
                pe.wait_ge(pr_ok, s + 1)
                for k in range(HALF):
                    own = slice(P * k, P * k + P)
                    last = pe.transpose(ps_t[:, own], pr[:, own], ident[:, :])
                last.then_inc(t_ps, 1)
                if v or j == 2:
                    pe.wait_ge(v_lo_ok, s + 2)
                if v:
                    if ahead == 0:
                        pe.wait_ge(wv_lo_ok, g + 2)
                    values(ahead)
                pe.wait_ge(pt_lo_ok, s + 1)
                pe.wait_ge(at_lo_ok, s)
                for k in range(HALF):
                    own = slice(P * k, P * k + P)
                    t, hp = HALF * (j // 2) + k, j % 2
                    head = slice(P * hp, P * hp + P)
                    last = three_passes(pe, ps_a[:, own], [((v_hi[:, t, head], v_lo[:, t, head]), (pt_hi[:, own], pt_lo[:, own]))])
                last.then_inc(a_ps, 1)
                if o:
                    if ahead == 0:
                        pe.wait_ge(wo_lo_ok, g + 1)
                    pe.wait_ge(acc_ok, B + 2 * s - 4)
                    output(ahead)

            slot(0, 0, 0, o=False, start=True)
            slot(1, 1, 0, o=False, start=True)
            with pe.Fori(0, PAIRS - 1) as i:
                slot(4 * i + 2, 2, i)
                slot(4 * i + 3, 3, i)
                slot(4 * i + 4, 0, i + 1)
                slot(4 * i + 5, 1, i + 1)
            slot(STEPS - 2, 2, PAIRS - 1, v=False)
            slot(STEPS - 1, 3, PAIRS - 1, qk=False, v=False)

            def x1_transposes(h):
                for t in range(HALF * h, HALF * h + HALF):
                    pe.wait_ge(x1n_ok, t + 1)
                    if t >= HALF + 2:
                        pe.wait_ge(x1t_lo_ok, t - 1)
                    for c in range(DC):
                        last = pe.transpose(ps_x1[t][:, P * c:P * c + P], acc[:, t, P * c:P * c + P], ident[:, :])
                    last.then_inc(x1t_ps, 1)

            def tokens(t):
                own = slice(P * t, P * t + P)
                return [(xt_hi[:, c, own], xt_lo[:, c, own]) for c in range(DC)]

            def lora(h):
                for t in range(HALF * h, HALF * h + HALF):
                    pe.wait_ge(x1t_lo_ok, t + 1)
                    n = t % HALF
                    mm = three_passes(pe, ps_lora[n // 2][:, LW * (n % 2):LW * (n % 2) + LW],
                                      [(tok, (lora_hi[:, c, :], lora_lo[:, c, :])) for c, tok in enumerate(tokens(t))])
                    if n % 2:
                        mm.then_inc(lora_ps, 1)

            def base(h):
                for t in range(HALF * h, HALF * h + HALF):
                    if h == 1:
                        pe.wait_ge(y_ok, t - 3)
                    mm = three_passes(pe, ps_base[t % 4][:, :],
                                      [(tok, (base_hi[:, c, :], base_lo[:, c, :])) for c, tok in enumerate(tokens(t))],
                                      last=False)

            def hw_transposes(h):
                pe.wait_ge(hw_ok, 2 * h + 2)
                pe.wait_ge(x1t_lo_ok, 2 * HALF)
                if h == 1:
                    pe.wait_ge(hwt_lo_ok, 1)
                for k in range(HALF):
                    last = pe.transpose(ps_t[:, P * k:P * k + P], hw[:, k, :], ident[:, :])
                last.then_inc(hwt_ps, 1)

            def up(h):
                pe.wait_ge(hwt_lo_ok, h + 1)
                for t in range(HALF * h, HALF * h + HALF):
                    own = slice(P * (t % HALF), P * (t % HALF) + P)
                    three_passes(pe, ps_base[t % 4][:, :], [((pt_hi[:, own], pt_lo[:, own]), (up_hi[:, :], up_lo[:, :]))],
                                 first=False).then_inc(y_ps, 1)

            pe.wait_ge(at_lo_ok, STEPS)
            pe.wait_ge(acc_ok, B + 2 * STEPS - 4)
            output(2)
            x1_transposes(0)
            pe.wait_ge(acc_ok, B + 2 * STEPS - 2)
            output(3)
            pe.wait_ge(ffn_lo_ok, 3)
            lora(0)
            pe.wait_ge(acc_ok, B + 2 * STEPS)
            base(0)
            x1_transposes(1)
            hw_transposes(0)
            up(0)
            pe.wait_ge(hw_ok, 2)
            lora(1)
            base(1)
            hw_transposes(1)
            up(1)


def _layouts(x, ctx_4096, mask_BxSxS2_bk0, g_xattn, g_ffn, L0_xattn_position_bias, L0_xattn_ln_weight,
             L0_xattn_w_q, L0_xattn_w_k, L0_xattn_w_v, L0_xattn_w_out, L0_ffn_W_base, L0_ffn_b_base,
             L0_ffn_W_router, L0_ffn_A, L0_ffn_B):
    import numpy as np
    a = np.asarray

    def chunks(w, n):
        w = a(w)
        return w.reshape(-1, n, DC, P).transpose(0, 3, 2, 1).reshape(-1, P, DC * n)

    lora_in = np.concatenate([a(L0_ffn_A).reshape(ER, D), a(L0_ffn_W_router)], axis=0)
    return {
        "x": a(x).transpose(1, 0, 2),
        "ctx_t": a(ctx_4096).reshape(2, W, DC, P).transpose(0, 3, 2, 1),
        "mask": a(mask_BxSxS2_bk0).transpose(1, 0, 2),
        "gates": np.broadcast_to(np.concatenate([a(g_xattn), a(g_ffn)]), (P, 2)),
        "bias": a(L0_xattn_position_bias).reshape(PAIRS, 2, P, P).transpose(0, 2, 1, 3),
        "ln_w": a(L0_xattn_ln_weight).reshape(DC, P).T,
        "w_qk": np.concatenate([chunks(L0_xattn_w_q, P), chunks(L0_xattn_w_k, P)], axis=2),
        "w_v": chunks(L0_xattn_w_v, 2 * P),
        "w_o": a(L0_xattn_w_out).reshape(D, PAIRS, 2, P).transpose(1, 3, 2, 0).reshape(PAIRS, P, 2 * D),
        "w_base": chunks(L0_ffn_W_base, D)[0],
        "w_lora": chunks(lora_in, ER + E)[0],
        "w_up": a(L0_ffn_B).transpose(0, 2, 1).reshape(ER, D),
        "b_base": np.broadcast_to(a(L0_ffn_b_base), (P, D)),
    }


def kernel(**inputs):
    import numpy as np
    import concourse.bacc as bacc
    from concourse.bass_utils import run_bass_kernel_spmd

    nc = bacc.Bacc("TRN2", target_bir_lowering=False, num_devices=1)
    arrays, args = {}, {}
    for name, array in _layouts(**inputs).items():
        array = np.ascontiguousarray(array)
        arrays[f"in_{name}"] = array
        args[name] = nc.dram_tensor(f"in_{name}", array.shape, mybir.dt.from_np(array.dtype), kind="ExternalInput").ap()
    args["out"] = nc.dram_tensor("out_y", (P, B, D), F32, kind="ExternalOutput").ap()
    flamingo_block(nc, **args)
    result = run_bass_kernel_spmd(nc, [arrays], core_ids=[0])
    return np.ascontiguousarray(result.results[0]["out_y"].transpose(1, 0, 2))
```

```python
from contextlib import ExitStack

import concourse.bass as bass
from concourse import mybir

F32 = mybir.dt.float32
F32R = mybir.dt.float32r
U8 = mybir.dt.uint8
U32 = mybir.dt.uint32
ALU = mybir.AluOpType
ACT = mybir.ActivationFunctionType
AX = mybir.AxisListType

P = 128
B = 8
D = 512
DC = D // P
H = 32
HALF = B // 2
W = HALF * P
PAIRS = H // 2
STEPS = 4 * PAIRS
E = 8
R = 16
ER = E * R
EPS = 1e-5
SCALING = 32 / R
MASKED = 1e30


def flamingo_block(nc, x, ctx_t, mask, gates, bias, ln_w, w_qk, w_v, w_o, w_base, w_lora, w_up, b_base, out):
    stack = ExitStack()
    with stack:
        def sb(name, shape, dt=F32):
            return stack.enter_context(nc.sbuf_tensor(name, shape, dt))

        def sem(name):
            return stack.enter_context(nc.semaphore(name))

        acc = sb("acc", [P, B, D])
        res = sb("res", [P, B, D])
        xt_hi = sb("xt_hi", [P, DC, B * P], F32R)
        xt_lo = sb("xt_lo", [P, DC, B * P], F32R)
        ct_hi = sb("ct_hi", [P, DC, B * P], F32R)
        ct_lo = sb("ct_lo", [P, DC, B * P], F32R)
        v_hi = sb("v_hi", [P, B, 2 * P], F32R)
        v_lo = sb("v_lo", [P, B, 2 * P], F32R)
        at_hi = sb("at_hi", [P, 4, W], F32R)
        at_lo = sb("at_lo", [P, 4, W], F32R)
        raw_qk = sb("raw_qk", [P, 2, 2 * D])
        raw_v = sb("raw_v", [P, 2 * D])
        raw_o = sb("raw_o", [P, 2 * D])
        wqk_hi = sb("wqk_hi", [P, 2, 2 * D], F32R)
        wqk_lo = sb("wqk_lo", [P, 2, 2 * D], F32R)
        wv_hi = sb("wv_hi", [P, DC, 2 * P], F32R)
        wv_lo = sb("wv_lo", [P, DC, 2 * P], F32R)
        wo_hi = sb("wo_hi", [P, 2, D], F32R)
        wo_lo = sb("wo_lo", [P, 2, D], F32R)
        q_hi = sb("q_hi", [P, W], F32R)
        q_lo = sb("q_lo", [P, W], F32R)
        k_hl = sb("k_hl", [P, HALF, 2, P], F32R)
        sc = sb("sc", [P, W])
        pr = sb("pr", [P, W])
        pt_hl = sb("pt_hl", [P, HALF, 2, P], F32R)
        at_part = sb("at_part", [P, HALF, P])
        at_full = sb("at_full", [P, HALF, P])
        bias_sb = sb("bias_sb", [P, 2, P])
        bm = sb("bm", [P, HALF, P])
        mask8 = sb("mask8", [P, B, P], U8)
        mneg = sb("mneg", [P, B, P])
        allowed = sb("allowed", [P, B])
        ident = sb("ident", [P, P])
        lnw = sb("lnw", [P, DC])
        gate = sb("gate", [P, 2])
        tg = sb("tg", [P, 2])
        half_pow = sb("half_pow", [P, 2, HALF])
        stats = sb("stats", [P, B, 6])
        mv = sb("mv", [P, B, 2])
        scales = sb("scales", [P, 2, B])
        shift = sb("shift", [P, B])
        nmax = sb("nmax", [P, HALF])
        sums = sb("sums", [P, HALF])
        rinv = sb("rinv", [P, HALF])
        expert = sb("expert", [P, E])
        lg = sb("lg", [P, HALF, E])
        lmax = sb("lmax", [P, HALF])
        lsum = sb("lsum", [P, HALF])
        linv = sb("linv", [P, HALF])
        top = sb("top", [P, HALF, 8])
        top_i = sb("top_i", [P, HALF, 8], U32)
        top_f = sb("top_f", [P, HALF, 2])
        tw = sb("tw", [P, HALF, 2])
        hot = sb("hot", [P, 2, HALF, E])
        comb = sb("comb", [P, HALF, E])

        ps_q, ps_k, ps_t, ps_v, ps_o0, ps_o1 = [
            stack.enter_context(nc.psum_tensor(f"ps_{n}", [P, W], F32)) for n in ("q", "k", "t", "v", "o0", "o1")]
        ps_w = stack.enter_context(nc.psum_tensor("ps_w", [P, HALF, 2, P], F32))
        ps_w0 = ps_w[:, 0:2, :, :].rearrange("p b h n -> p (b h n)")
        ps_w1 = ps_w[:, 2:4, :, :].rearrange("p b h n -> p (b h n)")
        ps_o = [ps_o0, ps_o1]
        ps_x = [[ps_w0, ps_t, ps_o0, ps_o1],
                [ps_w1, ps_t, ps_o0, ps_o1]]
        ps_x1 = [ps_t, ps_q, ps_w0, ps_v, ps_t, ps_o1, ps_t, ps_o1]
        ps_lora = [ps_k, ps_q]
        ps_base = [ps_w0, ps_v, ps_w1, ps_o0]

        x_in = [sem("x_in0"), sem("x_in1")]
        ctx_in = [sem("ctx_in0"), sem("ctx_in1")]
        mask_in, small_in, bb_in = sem("mask_in"), sem("small_in"), sem("bb_in")
        wqk_in = [sem("wqk_in0"), sem("wqk_in1")]
        wv_in, wo_in, bias_in = sem("wv_in"), sem("wo_in"), sem("bias_in")
        lora_in, base_in, up_in = sem("lora_in"), sem("base_in"), sem("up_in")
        stored = sem("stored")
        ident_zero, ident_ok, consts_ok, pool_chain = sem("ident_zero"), sem("ident_ok"), sem("consts_ok"), sem("pool_chain")
        mneg_ok, allowed_ok, tanh_ok = sem("mneg_ok"), sem("allowed_ok"), sem("tanh_ok")
        bn_ok, mv_ok, scales_ok, xr_ok, ln_ok = [sem(n) for n in ("bn_ok", "mv_ok", "scales_ok", "xr_ok", "ln_ok")]
        xr_used, xt_hi_ok, xt_lo_ok = sem("xr_used"), sem("xt_hi_ok"), sem("xt_lo_ok")
        ct_hi_ok, ct_lo_ok = sem("ct_hi_ok"), sem("ct_lo_ok")
        wqk_hi_ok = [sem("wqk_hi_ok0"), sem("wqk_hi_ok1")]
        wqk_lo_ok = [sem("wqk_lo_ok0"), sem("wqk_lo_ok1")]
        wv_hi_ok, wv_lo_ok, wo_hi_ok, wo_lo_ok = sem("wv_hi_ok"), sem("wv_lo_ok"), sem("wo_hi_ok"), sem("wo_lo_ok")
        q_ps, k_ps, s_ps, t_ps, v_ps, a_ps, o_ps = [sem(n) for n in ("q_ps", "k_ps", "s_ps", "t_ps", "v_ps", "a_ps", "o_ps")]
        q_hi_ok, q_lo_ok, k_hi_ok, k_lo_ok = [sem(n) for n in ("q_hi_ok", "q_lo_ok", "k_hi_ok", "k_lo_ok")]
        pt_hi_ok, pt_lo_ok, v_hi_ok, v_lo_ok = [sem(n) for n in ("pt_hi_ok", "pt_lo_ok", "v_hi_ok", "v_lo_ok")]
        at_part_ok, at_full_ok, at_hi_ok, at_lo_ok = [sem(n) for n in ("at_part_ok", "at_full_ok", "at_hi_ok", "at_lo_ok")]
        bm_ok, biased, scored, nmax_ok, exp_ok, inv_ok, pr_ok, acc_ok = [
            sem(n) for n in ("bm_ok", "biased", "scored", "nmax_ok", "exp_ok", "inv_ok", "pr_ok", "acc_ok")]
        bn1_ok, mv1_ok, rstd1_ok, x1n_ok = [sem(n) for n in ("bn1_ok", "mv1_ok", "rstd1_ok", "x1n_ok")]
        x1t_ps, x1t_hi_ok, x1t_lo_ok = sem("x1t_ps"), sem("x1t_hi_ok"), sem("x1t_lo_ok")
        bg_ok, x1b_ok = sem("bg_ok"), sem("x1b_ok")
        ffn_hi_ok, ffn_lo_ok = sem("ffn_hi_ok"), sem("ffn_lo_ok")
        lora_ps, base_ps, route, lexp_ok, hw_ok = [sem(n) for n in ("lora_ps", "base_ps", "route", "lexp_ok", "hw_ok")]
        hwt_ps, hwt_hi_ok, hwt_lo_ok, y_ps, y_ok = [sem(n) for n in ("hwt_ps", "hwt_hi_ok", "hwt_lo_ok", "y_ps", "y_ok")]

        bb = sc
        ctx_raw = res[:, :, :].rearrange("p b d -> p (b d)").rearrange("p (h c n) -> p h c n", h=2, c=DC)
        xr_buf = [sc[:, :], pr[:, :], raw_o[:, 0:D], raw_o[:, D:2 * D]]
        base_hi = wqk_hi[:, :, :].rearrange("p h n -> p (h n)").rearrange("p (c n) -> p c n", c=DC)
        base_lo = wqk_lo[:, :, :].rearrange("p h n -> p (h n)").rearrange("p (c n) -> p c n", c=DC)
        LW = ER + E
        lora_hi = wv_hi[:, :, :].rearrange("p c n -> p (c n)")[:, 0:DC * LW].rearrange("p (c n) -> p c n", c=DC)
        lora_lo = wv_lo[:, :, :].rearrange("p c n -> p (c n)")[:, 0:DC * LW].rearrange("p (c n) -> p c n", c=DC)
        up_hi, up_lo = q_hi, q_lo
        hw = bm

        ROUTE_SHIFTED = 4
        ROUTE_STEPS = 24

        def wqk(w, hp, which, c):
            at = (which * DC + c) * P
            return w[:, hp, at:at + P]

        def three_passes(pe, dst, pairs, first=True, last=True):
            n, total = 0, 3 * len(pairs)
            for (l_hi, l_lo), (r_hi, r_lo) in pairs:
                for a, b in ((l_hi, r_hi), (l_hi, r_lo), (l_lo, r_hi)):
                    mm = pe.matmul(dst, a, b, start=first and n == 0, stop=last and n == total - 1)
                    n += 1
            return mm

        def by_batch(bank):
            return bank[:, :].rearrange("p (b n) -> p b n", b=HALF)

        def batches(i):
            return (2 * i, 2 * i + 1)

        block = stack.enter_context(nc.Block())

        @block.sync
        def _(sp):
            sp.dma_start(acc[:, 0:HALF, :], x[:, 0:HALF, :]).then_inc(x_in[0], 16)
            sp.dma_start(raw_v[:, :], w_v[0, :, :]).then_inc(wv_in, 16)
            sp.dma_start(acc[:, HALF:B, :], x[:, HALF:B, :]).then_inc(x_in[1], 16)
            sp.dma_start(raw_qk[:, 0, :], w_qk[0, :, :]).then_inc(wqk_in[0], 16)
            sp.dma_start(raw_qk[:, 1, :], w_qk[1, :, :]).then_inc(wqk_in[1], 16)
            sp.dma_start(mask8[:, :, :], mask).then_inc(mask_in, 16)
            sp.dma_start(bias_sb[:, :, :], bias[0, :, :, :]).then_inc(bias_in, 16)
            sp.wait_ge(xr_used, B)
            sp.dma_start(raw_o[:, :], w_o[0, :, :]).then_inc(wo_in, 16)
            with sp.Fori(0, PAIRS - 1) as i:
                sp.wait_ge(wv_lo_ok, i + 1)
                sp.dma_start(raw_v[:, :], w_v[i + 1, :, :]).then_inc(wv_in, 16)
                for hp in range(2):
                    sp.wait_ge(wqk_lo_ok[hp], i + 1)
                    sp.dma_start(raw_qk[:, hp, :], w_qk[2 * i + (2 + hp), :, :]).then_inc(wqk_in[hp], 16)
                sp.wait_ge(wo_lo_ok, i + 1)
                sp.dma_start(raw_o[:, :], w_o[i + 1, :, :]).then_inc(wo_in, 16)
                sp.wait_ge(bm_ok, 4 * i + 4)
                sp.dma_start(bias_sb[:, :, :], bias[i + 1, :, :, :]).then_inc(bias_in, 16)
            sp.wait_ge(wv_lo_ok, PAIRS)
            sp.dma_start(raw_v[:, 0:DC * LW], w_lora).then_inc(lora_in, 16)
            sp.wait_ge(wqk_lo_ok[0], PAIRS)
            sp.wait_ge(wqk_lo_ok[1], PAIRS)
            sp.dma_start(raw_qk[:, :, :].rearrange("p h n -> p (h n)"), w_base).then_inc(base_in, 16)
            sp.wait_ge(wo_lo_ok, PAIRS)
            sp.dma_start(raw_o[:, 0:D], w_up).then_inc(up_in, 16)
            sp.wait_ge(exp_ok, STEPS)
            sp.dma_start(bb[:, :], b_base).then_inc(bb_in, 16)
            for t in range(B):
                sp.wait_ge(y_ok, t + 1)
                sp.dma_start(out[:, t, :], res[:, t, :]).then_inc(stored, 16)
            sp.wait_ge(stored, 16 * B)

        @block.gpsimd
        def _(pool):
            pool.memset(ident[:, :], 0.0).then_inc(ident_zero, 1)
            pool.wait_ge(ident_zero, 1)
            pool.affine_select(out=ident[:, :], in_=ident[:, :], compare_op=ALU.not_equal, fill=1.0,
                               base=0, pattern=[[-1, P]], channel_multiplier=1).then_inc(ident_ok, 1)
            for e in range(E):
                pool.memset(expert[:, e:e + 1], float(e)).then_inc(consts_ok, 1)
            pool.memset(half_pow[:, :, :], -0.5).then_inc(consts_ok, 1)
            pool.wait_ge(consts_ok, E + 1)
            steps = [0]

            def link(op):
                op.then_inc(pool_chain, 1)
                steps[0] += 1
                pool.wait_ge(pool_chain, steps[0])

            for h in range(2):
                own = slice(HALF * h, HALF * h + HALF)
                pool.wait_ge(mv_ok, HALF * h + HALF)
                mean, var = mv[:, own, 0], mv[:, own, 1]
                link(pool.tensor_scalar(scales[:, 0, own], var, EPS, 0.0, ALU.add, ALU.add))
                link(pool.tensor_scalar(scales[:, 1, own], scales[:, 0, own], EPS, 0.0, ALU.mult, ALU.add))
                link(pool.tensor_tensor(scales[:, 1, own], scales[:, 1, own], var, ALU.add))
                link(pool.tensor_tensor(scales[:, :, own], scales[:, :, own], half_pow[:, :, :], ALU.pow))
                link(pool.tensor_tensor(shift[:, own], mean, scales[:, 1, own], ALU.mult))
                pool.tensor_scalar(shift[:, own], shift[:, own], -1.0, 0.0, ALU.mult, ALU.add).then_inc(scales_ok, 1)
            pool.wait_ge(mask_in, 16)
            pool.tensor_scalar(mneg[:, :, :], mask8[:, :, :], -1.0, MASKED, ALU.add, ALU.mult).then_inc(mneg_ok, 1)
            pool.wait_ge(mneg_ok, 1)

            def mask_step(s, j, g):
                if j == 0:
                    pool.wait_ge(bias_in, 16 * g + 16)
                own = slice(HALF * (j // 2), HALF * (j // 2) + HALF)
                head_bias = bias_sb[:, j % 2:j % 2 + 1, :].to_broadcast([P, HALF, P])
                pool.tensor_tensor(bm[:, :, :], head_bias, mneg[:, own, :], ALU.add).then_inc(bm_ok, 1)

            def slot(s, j, g, following=True):
                if following:
                    pool.wait_ge(biased, s + 1)
                    mask_step(s + 1, (j + 1) % 4, g + 1 if j == 3 else g)
                pool.wait_ge(at_hi_ok, s + 1)
                pool.tensor_tensor(at_lo[:, j, :], at_full[:, :, :].rearrange("p b n -> p (b n)"),
                                   at_hi[:, j, :].bitcast(F32), ALU.subtract).then_inc(at_lo_ok, 1)

            mask_step(0, 0, 0)
            slot(0, 0, 0)
            slot(1, 1, 0)
            with pool.Fori(0, PAIRS - 1) as i:
                slot(4 * i + 2, 2, i)
                slot(4 * i + 3, 3, i)
                slot(4 * i + 4, 0, i + 1)
                slot(4 * i + 5, 1, i + 1)
            slot(STEPS - 2, 2, PAIRS - 1)
            slot(STEPS - 1, 3, PAIRS - 1, following=False)

            for h in range(2):
                own = slice(HALF * h, HALF * h + HALF)
                pool.wait_ge(mv1_ok, HALF * h + HALF)
                link(pool.tensor_scalar(scales[:, 0, own], mv[:, own, 1], EPS, 0.0, ALU.add, ALU.add))
                pool.tensor_tensor(scales[:, 0, own], scales[:, 0, own], half_pow[:, 0, :], ALU.pow).then_inc(rstd1_ok, 1)
                if h == 0:
                    pool.wait_ge(bg_ok, 1)
                pool.wait_ge(x1n_ok, HALF * h + HALF)
                for t in range(HALF * h, HALF * h + HALF):
                    pool.tensor_tensor(acc[:, t, :], acc[:, t, :], bb[:, :], ALU.add).then_inc(x1b_ok, 1)

        @block.scalar
        def _(act):
            act.dma_start(ctx_raw[:, 0, :, :], ctx_t[0, :, :, :]).then_inc(ctx_in[0], 16)
            act.dma_start(lnw[:, :], ln_w).then_inc(small_in, 16)
            act.dma_start(gate[:, :], gates).then_inc(small_in, 16)
            act.dma_start(ctx_raw[:, 1, :, :], ctx_t[1, :, :, :]).then_inc(ctx_in[1], 16)

            def ctx_part(h):
                act.wait_ge(ctx_in[h], 16)
                act.activation(ct_hi[:, :, W * h:W * h + W], ctx_raw[:, h, :, :], ACT.Copy).then_inc(ct_hi_ok, 1)

            def split_wqk(hp, g):
                act.wait_ge(wqk_in[hp], 16 * g + 16)
                act.activation(wqk_hi[:, hp, :], raw_qk[:, hp, :], ACT.Copy).then_inc(wqk_hi_ok[hp], 1)

            def split_wv(g):
                act.wait_ge(wv_in, 16 * g + 16)
                act.activation(wv_hi[:, :, :], raw_v[:, :], ACT.Copy).then_inc(wv_hi_ok, 1)

            def split_wo(g):
                act.wait_ge(wo_in, 16 * g + 16)
                act.activation(wo_hi[:, :, :], raw_o[:, :], ACT.Copy).then_inc(wo_hi_ok, 1)

            def split_q(s):
                act.wait_ge(q_ps, s + 1)
                act.activation(q_hi[:, :], ps_q[:, :], ACT.Copy).then_inc(q_hi_ok, 1)

            def split_k(s):
                act.wait_ge(k_ps, s + 1)
                act.activation(k_hl[:, :, 0, :], by_batch(ps_k), ACT.Copy).then_inc(k_hi_ok, 1)

            def split_v(u, i):
                act.wait_ge(v_ps, u + 1)
                act.activation(v_hi[:, 2 * i:2 * i + 2, :], ps_v[:, :], ACT.Copy).then_inc(v_hi_ok, 1)

            def scale_tokens(h):
                act.wait_ge(scales_ok, h + 1)
                for t in range(HALF * h, HALF * h + HALF):
                    if h == 1:
                        act.wait_ge(xr_used, t - HALF + 1)
                    act.activation(xr_buf[t % HALF], acc[:, t, :], ACT.Identity, bias=shift[:, t:t + 1],
                                   scale=scales[:, 1, t:t + 1]).then_inc(xr_ok, 1)

            def token_hi(h):
                act.wait_ge(xr_used, HALF * h + HALF)
                for c in range(DC):
                    act.activation(xt_hi[:, c, W * h:W * h + W], ps_x[h][c][:, :], ACT.Copy,
                                   scale=lnw[:, c:c + 1]).then_inc(xt_hi_ok, 1)

            ctx_part(0)
            split_wv(0)
            scale_tokens(0)
            split_wqk(0, 0)
            split_v(0, 0)
            act.wait_ge(small_in, 32)
            token_hi(0)
            scale_tokens(1)
            split_v(1, 1)
            split_k(0)
            act.activation(tg[:, :], gate[:, :], ACT.Tanh).then_inc(tanh_ok, 1)
            ctx_part(1)
            split_q(0)
            split_wqk(1, 0)
            token_hi(1)

            def slot(s, j, g, qk=True, v=True):
                if j == 2 and v:
                    act.wait_ge(v_ps, s + 2)
                    split_wv(g + 1)
                act.wait_ge(nmax_ok, s + 1)
                for k in range(HALF):
                    own = slice(P * k, P * k + P)
                    last = act.activation(pr[:, own], sc[:, own], ACT.Exp, bias=nmax[:, k:k + 1], accum_out=sums[:, k:k + 1])
                last.then_inc(exp_ok, 1)
                if qk:
                    split_q(s + 1)
                if j == 2:
                    split_wo(g)
                if qk:
                    split_k(s + 1)
                act.wait_ge(t_ps, s + 1)
                act.activation(pt_hl[:, :, 0, :], by_batch(ps_t), ACT.Copy).then_inc(pt_hi_ok, 1)
                if j >= 2 and v:
                    split_wqk(j - 2, g + 1)
                if v:
                    split_v(s + 2, (j + 2) % 4)
                act.wait_ge(a_ps, s + 1)
                act.activation(at_part[:, :, :], ps_w[:, :, 1, :], ACT.Copy).then_inc(at_part_ok, 1)
                act.wait_ge(at_full_ok, s + 1)
                act.activation(at_hi[:, j, :], at_full[:, :, :], ACT.Copy).then_inc(at_hi_ok, 1)

            slot(0, 0, 0)
            slot(1, 1, 0)
            with act.Fori(0, PAIRS - 1) as i:
                slot(4 * i + 2, 2, i)
                slot(4 * i + 3, 3, i)
                slot(4 * i + 4, 0, i + 1)
                slot(4 * i + 5, 1, i + 1)
            act.wait_ge(lora_in, 16)
            act.activation(lora_hi, raw_v[:, 0:DC * LW], ACT.Copy).then_inc(ffn_hi_ok, 1)
            slot(STEPS - 2, 2, PAIRS - 1, v=False)
            act.wait_ge(base_in, 16)
            act.activation(base_hi, raw_qk[:, :, :].rearrange("p h n -> p (h n)"), ACT.Copy).then_inc(ffn_hi_ok, 1)
            slot(STEPS - 1, 3, PAIRS - 1, qk=False, v=False)
            act.wait_ge(up_in, 16)
            act.activation(up_hi[:, :], raw_o[:, 0:D], ACT.Copy).then_inc(ffn_hi_ok, 1)

            def x1_hi(h):
                for t in range(HALF * h, HALF * h + HALF):
                    act.wait_ge(x1t_ps, t + 1)
                    act.activation(xt_hi[:, :, P * t:P * t + P], ps_x1[t][:, :], ACT.Copy).then_inc(x1t_hi_ok, 1)

            def router_exp(h):
                act.wait_ge(route, ROUTE_STEPS * h + ROUTE_SHIFTED)
                act.activation(lg[:, :, :], lg[:, :, :], ACT.Exp).then_inc(lexp_ok, 1)

            def hwt_hi(h):
                act.wait_ge(hwt_ps, h + 1)
                act.activation(pt_hl[:, :, 0, :], by_batch(ps_t), ACT.Copy).then_inc(hwt_hi_ok, 1)

            x1_hi(0)
            router_exp(0)
            x1_hi(1)
            hwt_hi(0)
            router_exp(1)
            hwt_hi(1)

        @block.vector
        def _(ve):
            def lo(dst, src, hi):
                return ve.tensor_tensor(dst, src, hi.bitcast(F32), ALU.subtract)

            def moments(batch_range, bn_sem, mv_sem):
                for t in batch_range:
                    ve.bn_stats(stats[:, t, :], acc[:, t, :]).then_inc(bn_sem, 1)
                for t in batch_range:
                    ve.wait_ge(bn_sem, t + 1)
                    ve.bn_aggr(mv[:, t, :], stats[:, t, :]).then_inc(mv_sem, 1)

            def start_sum(h):
                ve.wait_ge(tanh_ok, 1)
                ve.wait_ge(xr_ok, HALF * h + HALF)
                for t in range(HALF * h, HALF * h + HALF):
                    ve.tensor_scalar(res[:, t, :], acc[:, t, :], mv[:, t, 0:1], scales[:, 0, t:t + 1],
                                     ALU.subtract, ALU.mult).then_inc(ln_ok, 1)
                for t in range(HALF * h, HALF * h + HALF):
                    ve.wait_ge(ln_ok, t + 1)
                    ve.scalar_tensor_tensor(acc[:, t, :], res[:, t, :], tg[:, 0:1], acc[:, t, :],
                                            ALU.mult, ALU.add).then_inc(acc_ok, 1)

            def ctx_part(h):
                ve.wait_ge(ct_hi_ok, h + 1)
                lo(ct_lo[:, :, W * h:W * h + W], ctx_raw[:, h, :, :], ct_hi[:, :, W * h:W * h + W]).then_inc(ct_lo_ok, 1)

            def split_wqk(hp, g):
                ve.wait_ge(wqk_hi_ok[hp], g + 1)
                lo(wqk_lo[:, hp, :], raw_qk[:, hp, :], wqk_hi[:, hp, :]).then_inc(wqk_lo_ok[hp], 1)

            def split_wv(g):
                ve.wait_ge(wv_hi_ok, g + 1)
                lo(wv_lo[:, :, :], raw_v[:, :].rearrange("p (c n) -> p c n", c=DC), wv_hi[:, :, :]).then_inc(wv_lo_ok, 1)

            def split_wo(g):
                ve.wait_ge(wo_hi_ok, g + 1)
                lo(wo_lo[:, :, :], raw_o[:, :].rearrange("p (c n) -> p c n", c=2), wo_hi[:, :, :]).then_inc(wo_lo_ok, 1)

            def split_q(s):
                ve.wait_ge(q_hi_ok, s + 1)
                lo(q_lo[:, :], ps_q[:, :], q_hi[:, :]).then_inc(q_lo_ok, 1)

            def split_k(s):
                ve.wait_ge(k_hi_ok, s + 1)
                lo(k_hl[:, :, 1, :], by_batch(ps_k), k_hl[:, :, 0, :]).then_inc(k_lo_ok, 1)

            def split_v(u, i):
                ve.wait_ge(v_hi_ok, u + 1)
                own = slice(2 * i, 2 * i + 2)
                lo(v_lo[:, own, :], ps_v[:, :].rearrange("p (b n) -> p b n", b=2), v_hi[:, own, :]).then_inc(v_lo_ok, 1)

            def token_lo(h):
                for c in range(DC):
                    ve.wait_ge(xt_hi_ok, DC * h + c + 1)
                    own = slice(W * h, W * h + W)
                    ve.scalar_tensor_tensor(xt_lo[:, c, own], ps_x[h][c][:, :], lnw[:, c:c + 1],
                                            xt_hi[:, c, own].bitcast(F32), ALU.mult, ALU.subtract).then_inc(xt_lo_ok, 1)

            def accumulate(w, i):
                for n, t in enumerate(batches(i)):
                    ve.wait_ge(o_ps, 2 * w + (n + 1))
                    ve.scalar_tensor_tensor(acc[:, t, :], ps_o[n][:, :], tg[:, 0:1], acc[:, t, :],
                                            ALU.mult, ALU.add).then_inc(acc_ok, 1)

            ve.wait_ge(x_in[0], 16)
            moments(range(0, HALF), bn_ok, mv_ok)
            ctx_part(0)
            split_wv(0)
            ve.wait_ge(x_in[1], 16)
            moments(range(HALF, B), bn_ok, mv_ok)
            split_wqk(0, 0)
            split_v(0, 0)
            ve.wait_ge(small_in, 32)
            token_lo(0)
            split_v(1, 1)
            split_k(0)
            ctx_part(1)
            split_q(0)
            split_wqk(1, 0)
            ve.wait_ge(mask_in, 16)
            ve.tensor_reduce(allowed[:, :], mask8[:, :, :], AX.X, ALU.max).then_inc(allowed_ok, 1)
            token_lo(1)
            ve.wait_ge(allowed_ok, 1)

            def slot(s, j, g, qk=True, v=True, o=True, while_exp=None, while_pt=None, after_pt=None):
                ve.wait_ge(s_ps, s + 1)
                ve.wait_ge(bm_ok, s + 1)
                ve.tensor_tensor(by_batch(sc), ps_w[:, :, 1, :], bm[:, :, :], ALU.add).then_inc(biased, 1)
                ve.wait_ge(biased, s + 1)
                ve.tensor_tensor(by_batch(sc), ps_w[:, :, 0, :], by_batch(sc), ALU.add).then_inc(scored, 1)
                ve.wait_ge(scored, s + 1)
                ve.tensor_reduce(nmax[:, :], sc[:, :].rearrange("p (b k) -> p b k", b=HALF), AX.X, ALU.max,
                                 negate=True).then_inc(nmax_ok, 1)
                if j == 2 and v:
                    split_wv(g + 1)
                if while_exp:
                    while_exp()
                ve.wait_ge(exp_ok, s + 1)
                ve.reciprocal(rinv[:, :], sums[:, :]).then_inc(inv_ok, 1)
                ve.wait_ge(inv_ok, s + 1)
                for k in range(HALF):
                    own = slice(P * k, P * k + P)
                    t = HALF * (j // 2) + k
                    last = ve.tensor_scalar(pr[:, own], pr[:, own], rinv[:, k:k + 1], allowed[:, t:t + 1],
                                            ALU.mult, ALU.mult)
                last.then_inc(pr_ok, 1)
                if qk:
                    split_q(s + 1)
                if j == 2:
                    split_wo(g)
                if qk:
                    split_k(s + 1)
                if while_pt:
                    while_pt()
                ve.wait_ge(pt_hi_ok, s + 1)
                lo(pt_hl[:, :, 1, :], by_batch(ps_t), pt_hl[:, :, 0, :]).then_inc(pt_lo_ok, 1)
                if after_pt:
                    after_pt()
                if j >= 2 and v:
                    split_wqk(j - 2, g + 1)
                if v:
                    split_v(s + 2, (j + 2) % 4)
                ve.wait_ge(at_part_ok, s + 1)
                ve.tensor_tensor(at_full[:, :, :], ps_w[:, :, 0, :], at_part[:, :, :], ALU.add).then_inc(at_full_ok, 1)
                if o:
                    accumulate(s - 2, (j + 2) % 4)

            slot(0, 0, 0, o=False)
            start_sum(0)
            slot(1, 1, 0, o=False)
            start_sum(1)
            with ve.Fori(0, PAIRS - 1) as i:
                slot(4 * i + 2, 2, i)
                slot(4 * i + 3, 3, i)
                slot(4 * i + 4, 0, i + 1)
                slot(4 * i + 5, 1, i + 1)
            slot(STEPS - 2, 2, PAIRS - 1, v=False, o=False, after_pt=lambda: accumulate(STEPS - 4, 0))
            ve.wait_ge(ffn_hi_ok, 1)
            lo(lora_lo, raw_v[:, 0:DC * LW].rearrange("p (c n) -> p c n", c=DC), lora_hi).then_inc(ffn_lo_ok, 1)
            accumulate(STEPS - 3, 1)
            ve.wait_ge(acc_ok, B + 2 * (STEPS - 2))
            slot(STEPS - 1, 3, PAIRS - 1, qk=False, v=False, o=False,
                 while_exp=lambda: moments(range(0, 2), bn1_ok, mv1_ok),
                 while_pt=lambda: moments(range(2, HALF), bn1_ok, mv1_ok))

            def center1(h):
                ve.wait_ge(rstd1_ok, h + 1)
                for t in range(HALF * h, HALF * h + HALF):
                    ve.tensor_scalar(res[:, t, :], acc[:, t, :], mv[:, t, 0:1], scales[:, 0, t:t + 1],
                                     ALU.subtract, ALU.mult).then_inc(x1n_ok, 1)

            def x1_lo(h):
                for t in range(HALF * h, HALF * h + HALF):
                    ve.wait_ge(x1t_hi_ok, t + 1)
                    own = slice(P * t, P * t + P)
                    lo(xt_lo[:, :, own], ps_x1[t][:, :].rearrange("p (c n) -> p c n", c=DC),
                       xt_hi[:, :, own]).then_inc(x1t_lo_ok, 1)

            steps = [0]

            def link(op, wait=True):
                op.then_inc(route, 1)
                steps[0] += 1
                if wait:
                    ve.wait_ge(route, steps[0])

            def spread(ap, n):
                return ap.unsqueeze(2).to_broadcast([P, HALF, n])

            def routing(h):
                for n in range(2):
                    ve.wait_ge(lora_ps, 2 * h + n + 1)
                    logits = ps_lora[n][:, 0:2 * LW].rearrange("p (b n) -> p b n", b=2)[:, :, ER:LW]
                    link(ve.tensor_copy(lg[:, 2 * n:2 * n + 2, :], logits), wait=n == 1)
                link(ve.tensor_reduce(lmax[:, :], lg[:, :, :], AX.X, ALU.max))
                link(ve.tensor_tensor(lg[:, :, :], lg[:, :, :], spread(lmax[:, :], E), ALU.subtract))
                assert steps[0] == ROUTE_STEPS * h + ROUTE_SHIFTED
                ve.wait_ge(lexp_ok, h + 1)
                link(ve.tensor_reduce(lsum[:, :], lg[:, :, :], AX.X, ALU.add))
                link(ve.reciprocal(linv[:, :], lsum[:, :]))
                link(ve.tensor_tensor(lg[:, :, :], lg[:, :, :], spread(linv[:, :], E), ALU.mult))
                for k in range(HALF):
                    link(ve.max(top[:, k, :], lg[:, k, :]), wait=k == HALF - 1)
                for k in range(HALF):
                    link(ve.max_index(top_i[:, k, :], top[:, k, :], lg[:, k, :]), wait=k == HALF - 1)
                link(ve.tensor_copy(top_f[:, :, :], top_i[:, :, 0:2]), wait=False)
                link(ve.tensor_tensor(lsum[:, :], top[:, :, 0], top[:, :, 1], ALU.add))
                link(ve.reciprocal(linv[:, :], lsum[:, :]))
                link(ve.scalar_tensor_tensor(tw[:, :, :], top[:, :, 0:2], SCALING, spread(linv[:, :], 2), ALU.mult, ALU.mult))
                numbers = expert[:, :].unsqueeze(1).to_broadcast([P, HALF, E])
                for n in range(2):
                    link(ve.tensor_tensor(hot[:, n, :, :], numbers, spread(top_f[:, :, n], E), ALU.is_equal), wait=n == 1)
                for n in range(2):
                    link(ve.tensor_tensor(hot[:, n, :, :], hot[:, n, :, :], spread(tw[:, :, n], E), ALU.mult), wait=n == 1)
                link(ve.tensor_tensor(comb[:, :, :], hot[:, 0, :, :], hot[:, 1, :, :], ALU.add))
                assert steps[0] == ROUTE_STEPS * (h + 1)
                if h == 1:
                    ve.wait_ge(hwt_ps, 1)
                for n in range(2):
                    hidden = ps_lora[n][:, 0:2 * LW].rearrange("p (b n) -> p b n", b=2)[:, :, 0:ER]
                    weight = comb[:, 2 * n:2 * n + 2, :].unsqueeze(3).to_broadcast([P, 2, E, R])
                    ve.tensor_tensor(hw[:, 2 * n:2 * n + 2, :].rearrange("p b (e r) -> p b e r", e=E),
                                     hidden.rearrange("p b (e r) -> p b e r", e=E), weight, ALU.mult).then_inc(hw_ok, 1)

            def hwt_lo(h):
                ve.wait_ge(hwt_hi_ok, h + 1)
                lo(pt_hl[:, :, 1, :], by_batch(ps_t), pt_hl[:, :, 0, :]).then_inc(hwt_lo_ok, 1)

            def finish(h):
                for t in range(HALF * h, HALF * h + HALF):
                    ve.wait_ge(y_ps, t + 1)
                    ve.wait_ge(x1b_ok, t + 1)
                    ve.scalar_tensor_tensor(res[:, t, :], ps_base[t % 4][:, :], tg[:, 1:2], acc[:, t, :],
                                            ALU.mult, ALU.add).then_inc(y_ok, 1)

            center1(0)
            ve.wait_ge(bb_in, 16)
            ve.tensor_scalar(bb[:, :], bb[:, :], tg[:, 1:2], None, ALU.mult).then_inc(bg_ok, 1)
            ve.wait_ge(ffn_hi_ok, 3)
            lo(base_lo, raw_qk[:, :, :].rearrange("p h n -> p (h n)").rearrange("p (c n) -> p c n", c=DC), base_hi).then_inc(ffn_lo_ok, 1)
            lo(up_lo[:, :], raw_o[:, 0:D], up_hi[:, :]).then_inc(ffn_lo_ok, 1)
            x1_lo(0)
            accumulate(STEPS - 2, 2)
            accumulate(STEPS - 1, 3)
            ve.wait_ge(acc_ok, B + 2 * STEPS)
            moments(range(HALF, B), bn1_ok, mv1_ok)
            routing(0)
            center1(1)
            x1_lo(1)
            hwt_lo(0)
            finish(0)
            routing(1)
            hwt_lo(1)
            finish(1)

        @block.tensor
        def _(pe):
            def two_loads(pe, k, a_hi, a_lo, b_hl):
                pe.matmul(ps_w[:, k, :, :], a_hi, b_hl[:, k, :, :], start=True, stop=False)
                return pe.matmul(ps_w[:, k, 0, :], a_lo, b_hl[:, k, 0, :], start=False, stop=True)

            def project(dst, hp, which, token_hi, token_lo, half):
                own = slice(W * half, W * half + W)
                return three_passes(pe, dst, [((wqk(wqk_hi, hp, which, c), wqk(wqk_lo, hp, which, c)),
                                               (token_hi[:, c, own], token_lo[:, c, own])) for c in range(DC)])

            def queries(j):
                project(ps_q[:, :], j % 2, 0, xt_hi, xt_lo, j // 2).then_inc(q_ps, 1)

            def keys(j):
                project(ps_k[:, :], j % 2, 1, ct_hi, ct_lo, j // 2).then_inc(k_ps, 1)

            def values(i):
                for n, t in enumerate(batches(i)):
                    own = slice(P * t, P * t + P)
                    last = three_passes(pe, ps_v[:, 2 * P * n:2 * P * n + 2 * P],
                                        [((ct_hi[:, c, own], ct_lo[:, c, own]), (wv_hi[:, c, :], wv_lo[:, c, :]))
                                         for c in range(DC)])
                last.then_inc(v_ps, 1)

            def output(i):
                for n, t in enumerate(batches(i)):
                    own = slice(P * (t % HALF), P * (t % HALF) + P)
                    first = 2 * (t // HALF)
                    three_passes(pe, ps_o[n][:, :],
                                 [((at_hi[:, first + hp, own], at_lo[:, first + hp, own]),
                                   (wo_hi[:, hp, :], wo_lo[:, hp, :])) for hp in range(2)]).then_inc(o_ps, 1)

            def first_transposes(h):
                for t in range(HALF * h, HALF * h + HALF):
                    pe.wait_ge(xr_ok, t + 1)
                    for c in range(DC):
                        last = pe.transpose(ps_x[h][c][:, P * (t % HALF):P * (t % HALF) + P],
                                            xr_buf[t % HALF][:, P * c:P * c + P], ident[:, :])
                    last.then_inc(xr_used, 1)

            pe.wait_ge(ct_lo_ok, 1)
            pe.wait_ge(wv_lo_ok, 1)
            values(0)
            pe.wait_ge(ident_ok, 1)
            first_transposes(0)
            pe.wait_ge(v_lo_ok, 1)
            values(1)
            pe.wait_ge(wqk_lo_ok[0], 1)
            keys(0)
            pe.wait_ge(xt_lo_ok, DC)
            queries(0)
            first_transposes(1)

            def slot(s, j, g, qk=True, v=True, o=True, start=False, first=False, before_attention=None):
                nxt, ahead = (j + 1) % 4, (j + 2) % 4
                pe.wait_ge(q_lo_ok, s + 1)
                pe.wait_ge(k_lo_ok, s + 1)
                if not first:
                    pe.wait_ge(at_full_ok, s)
                for k in range(HALF):
                    own = slice(P * k, P * k + P)
                    last = two_loads(pe, k, q_hi[:, own], q_lo[:, own], k_hl)
                last.then_inc(s_ps, 1)
                if qk:
                    if nxt < 2:
                        pe.wait_ge(wqk_lo_ok[nxt], (g + 1 if j == 3 else g) + 1)
                    if start and j == 1:
                        pe.wait_ge(ct_lo_ok, 2)
                        pe.wait_ge(xt_lo_ok, 2 * DC)
                    queries(nxt)
                    keys(nxt)
                if start and j == 0:
                    pe.wait_ge(xt_lo_ok, 2 * DC)
                    pe.wait_ge(ct_lo_ok, 2)
                pe.wait_ge(pr_ok, s + 1)
                for k in range(HALF):
                    own = slice(P * k, P * k + P)
                    last = pe.transpose(ps_t[:, own], pr[:, own], ident[:, :])
                last.then_inc(t_ps, 1)
                if v or j == 2:
                    pe.wait_ge(v_lo_ok, s + 2)
                if v:
                    if ahead == 0:
                        pe.wait_ge(wv_lo_ok, g + 2)
                    values(ahead)
                if before_attention:
                    before_attention()
                pe.wait_ge(pt_lo_ok, s + 1)
                if not first:
                    pe.wait_ge(at_lo_ok, s)
                for k in range(HALF):
                    t, hp = HALF * (j // 2) + k, j % 2
                    head = slice(P * hp, P * hp + P)
                    last = two_loads(pe, k, v_hi[:, t, head], v_lo[:, t, head], pt_hl)
                last.then_inc(a_ps, 1)
                if o:
                    if ahead == 0:
                        pe.wait_ge(wo_lo_ok, g + 1)
                    pe.wait_ge(acc_ok, B + 2 * s - 4)
                    output(ahead)

            pe.wait_ge(xt_lo_ok, DC + 1)
            slot(0, 0, 0, o=False, start=True, first=True)
            slot(1, 1, 0, o=False, start=True)
            with pe.Fori(0, PAIRS - 1) as i:
                slot(4 * i + 2, 2, i)
                slot(4 * i + 3, 3, i)
                slot(4 * i + 4, 0, i + 1)
                slot(4 * i + 5, 1, i + 1)
            def output_60():
                pe.wait_ge(wo_lo_ok, PAIRS)
                pe.wait_ge(at_lo_ok, STEPS - 2)
                pe.wait_ge(acc_ok, B + 2 * (STEPS - 4))
                output(0)

            slot(STEPS - 2, 2, PAIRS - 1, v=False, o=False, before_attention=output_60)
            pe.wait_ge(acc_ok, B + 2 * (STEPS - 3))
            output(1)
            slot(STEPS - 1, 3, PAIRS - 1, qk=False, v=False, o=False)

            def x1_transposes(h):
                for t in range(HALF * h, HALF * h + HALF):
                    pe.wait_ge(x1n_ok, t + 1)
                    if t >= HALF + 2:
                        pe.wait_ge(x1t_lo_ok, t - 1)
                    for c in range(DC):
                        last = pe.transpose(ps_x1[t][:, P * c:P * c + P], res[:, t, P * c:P * c + P], ident[:, :])
                    last.then_inc(x1t_ps, 1)

            def tokens(t):
                own = slice(P * t, P * t + P)
                return [(xt_hi[:, c, own], xt_lo[:, c, own]) for c in range(DC)]

            def lora(h):
                for t in range(HALF * h, HALF * h + HALF):
                    pe.wait_ge(x1t_lo_ok, t + 1)
                    n = t % HALF
                    mm = three_passes(pe, ps_lora[n // 2][:, LW * (n % 2):LW * (n % 2) + LW],
                                      [(tok, (lora_hi[:, c, :], lora_lo[:, c, :])) for c, tok in enumerate(tokens(t))])
                    if n % 2:
                        mm.then_inc(lora_ps, 1)

            def base(h):
                for t in range(HALF * h, HALF * h + HALF):
                    if h == 1:
                        pe.wait_ge(y_ok, t - 3)
                    mm = three_passes(pe, ps_base[t % 4][:, :],
                                      [(tok, (base_hi[:, c, :], base_lo[:, c, :])) for c, tok in enumerate(tokens(t))],
                                      last=False)

            def hw_transposes(h):
                pe.wait_ge(hw_ok, 2 * h + 2)
                pe.wait_ge(x1t_lo_ok, 2 * HALF)
                if h == 1:
                    pe.wait_ge(hwt_lo_ok, 1)
                for k in range(HALF):
                    last = pe.transpose(ps_t[:, P * k:P * k + P], hw[:, k, :], ident[:, :])
                last.then_inc(hwt_ps, 1)

            def up(h):
                pe.wait_ge(hwt_lo_ok, h + 1)
                for t in range(HALF * h, HALF * h + HALF):
                    three_passes(pe, ps_base[t % 4][:, :], [((pt_hl[:, t % HALF, 0, :], pt_hl[:, t % HALF, 1, :]),
                                                             (up_hi[:, :], up_lo[:, :]))],
                                 first=False).then_inc(y_ps, 1)

            x1_transposes(0)
            pe.wait_ge(at_lo_ok, STEPS)
            pe.wait_ge(acc_ok, B + 2 * (STEPS - 2))
            output(2)
            pe.wait_ge(acc_ok, B + 2 * (STEPS - 1))
            output(3)
            pe.wait_ge(ffn_lo_ok, 3)
            lora(0)
            pe.wait_ge(acc_ok, B + 2 * STEPS)
            base(0)
            x1_transposes(1)
            hw_transposes(0)
            up(0)
            pe.wait_ge(hw_ok, 2)
            lora(1)
            base(1)
            hw_transposes(1)
            up(1)


def _layouts(x, ctx_4096, mask_BxSxS2_bk0, g_xattn, g_ffn, L0_xattn_position_bias, L0_xattn_ln_weight,
             L0_xattn_w_q, L0_xattn_w_k, L0_xattn_w_v, L0_xattn_w_out, L0_ffn_W_base, L0_ffn_b_base,
             L0_ffn_W_router, L0_ffn_A, L0_ffn_B):
    import numpy as np
    a = np.asarray

    def chunks(w, n):
        w = a(w)
        return w.reshape(-1, n, DC, P).transpose(0, 3, 2, 1).reshape(-1, P, DC * n)

    lora_in = np.concatenate([a(L0_ffn_A).reshape(ER, D), a(L0_ffn_W_router)], axis=0)
    return {
        "x": a(x).transpose(1, 0, 2),
        "ctx_t": a(ctx_4096).reshape(2, W, DC, P).transpose(0, 3, 2, 1),
        "mask": a(mask_BxSxS2_bk0).transpose(1, 0, 2),
        "gates": np.broadcast_to(np.concatenate([a(g_xattn), a(g_ffn)]), (P, 2)),
        "bias": a(L0_xattn_position_bias).reshape(PAIRS, 2, P, P).transpose(0, 2, 1, 3),
        "ln_w": a(L0_xattn_ln_weight).reshape(DC, P).T,
        "w_qk": np.concatenate([chunks(L0_xattn_w_q, P), chunks(L0_xattn_w_k, P)], axis=2),
        "w_v": chunks(L0_xattn_w_v, 2 * P),
        "w_o": a(L0_xattn_w_out).reshape(D, PAIRS, 2, P).transpose(1, 3, 2, 0).reshape(PAIRS, P, 2 * D),
        "w_base": chunks(L0_ffn_W_base, D)[0],
        "w_lora": chunks(lora_in, ER + E)[0],
        "w_up": a(L0_ffn_B).transpose(0, 2, 1).reshape(ER, D),
        "b_base": np.broadcast_to(a(L0_ffn_b_base), (P, D)),
    }


def kernel(**inputs):
    import numpy as np
    import concourse.bacc as bacc
    from concourse.bass_utils import run_bass_kernel_spmd

    nc = bacc.Bacc("TRN2", target_bir_lowering=False, num_devices=1)
    arrays, args = {}, {}
    for name, array in _layouts(**inputs).items():
        array = np.ascontiguousarray(array)
        arrays[f"in_{name}"] = array
        args[name] = nc.dram_tensor(f"in_{name}", array.shape, mybir.dt.from_np(array.dtype), kind="ExternalInput").ap()
    args["out"] = nc.dram_tensor("out_y", (P, B, D), F32, kind="ExternalOutput").ap()
    flamingo_block(nc, **args)
    result = run_bass_kernel_spmd(nc, [arrays], core_ids=[0])
    return np.ascontiguousarray(result.results[0]["out_y"].transpose(1, 0, 2))
```

```python
from contextlib import ExitStack

import concourse.bass as bass
from concourse import mybir

F32 = mybir.dt.float32
F32R = mybir.dt.float32r
U8 = mybir.dt.uint8
U32 = mybir.dt.uint32
ALU = mybir.AluOpType
ACT = mybir.ActivationFunctionType
AX = mybir.AxisListType

P = 128
B = 8
D = 512
DC = D // P
H = 32
HALF = B // 2
W = HALF * P
PAIRS = H // 2
STEPS = 4 * PAIRS
E = 8
R = 16
ER = E * R
EPS = 1e-5
SCALING = 32 / R
MASKED = 1e30

WARM_UP = 60


def flamingo_block(nc, x, ctx_t, mask, gates, bias, ln_w, w_qk, w_v, w_o, w_base, w_lora, w_up, b_base, out):
    stack = ExitStack()
    with stack:
        def sb(name, shape, dt=F32):
            return stack.enter_context(nc.sbuf_tensor(name, shape, dt))

        def sem(name):
            return stack.enter_context(nc.semaphore(name))

        acc = sb("acc", [P, B, D])
        res = sb("res", [P, B, D])
        xt_hi = sb("xt_hi", [P, DC, B * P], F32R)
        xt_lo = sb("xt_lo", [P, DC, B * P], F32R)
        ct_hi = sb("ct_hi", [P, DC, B * P], F32R)
        ct_lo = sb("ct_lo", [P, DC, B * P], F32R)
        v_hi = sb("v_hi", [P, B, 2 * P], F32R)
        v_lo = sb("v_lo", [P, B, 2 * P], F32R)
        at_hi = sb("at_hi", [P, 4, W], F32R)
        at_lo = sb("at_lo", [P, 4, W], F32R)
        raw_qk = sb("raw_qk", [P, 2, 2 * D])
        raw_v = sb("raw_v", [P, 2 * D])
        raw_o = sb("raw_o", [P, 2 * D])
        wqk_hi = sb("wqk_hi", [P, 2, 2 * D], F32R)
        wqk_lo = sb("wqk_lo", [P, 2, 2 * D], F32R)
        wv_hi = sb("wv_hi", [P, DC, 2 * P], F32R)
        wv_lo = sb("wv_lo", [P, DC, 2 * P], F32R)
        wo_hi = sb("wo_hi", [P, 2, D], F32R)
        wo_lo = sb("wo_lo", [P, 2, D], F32R)
        q_hi = sb("q_hi", [P, W], F32R)
        q_lo = sb("q_lo", [P, W], F32R)
        k_hl = sb("k_hl", [P, HALF, 2, P], F32R)
        sc = sb("sc", [P, W])
        pr = sb("pr", [P, W])
        pt_hl = sb("pt_hl", [P, HALF, 2, P], F32R)
        at_part = sb("at_part", [P, HALF, P])
        at_full = sb("at_full", [P, HALF, P])
        bias_sb = sb("bias_sb", [P, 2, P])
        bm = sb("bm", [P, HALF, P])
        mask8 = sb("mask8", [P, B, P], U8)
        mneg = sb("mneg", [P, B, P])
        allowed = sb("allowed", [P, B])
        ident = sb("ident", [P, P])
        lnw = sb("lnw", [P, DC])
        gate = sb("gate", [P, 2])
        tg = sb("tg", [P, 2])
        half_pow = sb("half_pow", [P, 2, HALF])
        stats = sb("stats", [P, B, 6])
        mv = sb("mv", [P, B, 2])
        scales = sb("scales", [P, 2, B])
        shift = sb("shift", [P, B])
        gated = sb("gated", [P, 2, B])
        nmax = sb("nmax", [P, HALF])
        sums = sb("sums", [P, HALF])
        rinv = sb("rinv", [P, HALF])
        expert = sb("expert", [P, E])
        lg = sb("lg", [P, HALF, E])
        lmax = sb("lmax", [P, HALF])
        lsum = sb("lsum", [P, HALF])
        linv = sb("linv", [P, HALF])
        top = sb("top", [P, HALF, 8])
        top_i = sb("top_i", [P, HALF, 8], U32)
        top_f = sb("top_f", [P, HALF, 2])
        tw = sb("tw", [P, HALF, 2])
        hot = sb("hot", [P, 2, HALF, E])
        comb = sb("comb", [P, HALF, E])

        ps_q, ps_k, ps_t, ps_v, ps_o0, ps_o1 = [
            stack.enter_context(nc.psum_tensor(f"ps_{n}", [P, W], F32)) for n in ("q", "k", "t", "v", "o0", "o1")]
        ps_w = stack.enter_context(nc.psum_tensor("ps_w", [P, HALF, 2, P], F32))
        ps_w0 = ps_w[:, 0:2, :, :].rearrange("p b h n -> p (b h n)")
        ps_w1 = ps_w[:, 2:4, :, :].rearrange("p b h n -> p (b h n)")
        ps_o = [ps_o0, ps_o1]
        ps_x = [[ps_w0, ps_t, ps_o0, ps_o1],
                [ps_t, ps_v, ps_o0, ps_o1]]
        ps_last = [ps_v, ps_k, ps_q, ps_o1]
        ps_x1 = [ps_t, ps_o0, ps_w0, ps_t, ps_q, ps_w1, ps_o0, ps_t]
        ps_lora = [ps_w1, ps_o0]
        ps_base = [ps_w0, ps_v, ps_o1, ps_k]

        x_in = [sem("x_in0"), sem("x_in1")]
        ctx_in = [sem(f"ctx_in{n}") for n in range(3)]
        mask_in, small_in, bb_in = sem("mask_in"), sem("small_in"), sem("bb_in")
        wqk_in = [sem("wqk_in0"), sem("wqk_in1")]
        wv_in, wo_in, bias_in = sem("wv_in"), sem("wo_in"), sem("bias_in")
        lora_in, base_in, up_in = sem("lora_in"), sem("base_in"), sem("up_in")
        stored = sem("stored")
        ident_zero, ident_ok, consts_ok, pool_chain = sem("ident_zero"), sem("ident_ok"), sem("consts_ok"), sem("pool_chain")
        mneg_ok, allowed_ok, tanh_ok = sem("mneg_ok"), sem("allowed_ok"), sem("tanh_ok")
        bn_ok, mv_ok, scales_ok, xr_ok, gs_ok, ln_ok = [sem(n) for n in ("bn_ok", "mv_ok", "scales_ok", "xr_ok", "gs_ok", "ln_ok")]
        xr_used, xt_hi_ok, xt_lo_ok = sem("xr_used"), sem("xt_hi_ok"), sem("xt_lo_ok")
        ct_hi_ok, ct_lo_ok, ct_last_ok = sem("ct_hi_ok"), sem("ct_lo_ok"), sem("ct_last_ok")
        wqk_hi_ok = [sem("wqk_hi_ok0"), sem("wqk_hi_ok1")]
        wqk_lo_ok = [sem("wqk_lo_ok0"), sem("wqk_lo_ok1")]
        wv_hi_ok, wv_lo_ok, wo_hi_ok, wo_lo_ok = sem("wv_hi_ok"), sem("wv_lo_ok"), sem("wo_hi_ok"), sem("wo_lo_ok")
        q_ps, k_ps, s_ps, t_ps, v_ps, a_ps, o_ps = [sem(n) for n in ("q_ps", "k_ps", "s_ps", "t_ps", "v_ps", "a_ps", "o_ps")]
        q_hi_ok, q_lo_ok, k_hi_ok, k_lo_ok = [sem(n) for n in ("q_hi_ok", "q_lo_ok", "k_hi_ok", "k_lo_ok")]
        pt_hi_ok, pt_lo_ok, v_hi_ok, v_lo_ok = [sem(n) for n in ("pt_hi_ok", "pt_lo_ok", "v_hi_ok", "v_lo_ok")]
        at_part_ok, at_full_ok, at_hi_ok, at_lo_ok = [sem(n) for n in ("at_part_ok", "at_full_ok", "at_hi_ok", "at_lo_ok")]
        bm_ok, biased, scored, nmax_ok, exp_ok, inv_ok, pr_ok, acc_ok = [
            sem(n) for n in ("bm_ok", "biased", "scored", "nmax_ok", "exp_ok", "inv_ok", "pr_ok", "acc_ok")]
        bn1_ok, mv1_ok, rstd1_ok, x1n_ok = [sem(n) for n in ("bn1_ok", "mv1_ok", "rstd1_ok", "x1n_ok")]
        last_ps, x1t_ps, x1t_hi_ok, x1t_lo_ok = sem("last_ps"), sem("x1t_ps"), sem("x1t_hi_ok"), sem("x1t_lo_ok")
        bg_ok, x1b_ok = sem("bg_ok"), sem("x1b_ok")
        ffn_hi_ok, ffn_lo_ok, base_lo_ok = sem("ffn_hi_ok"), sem("ffn_lo_ok"), sem("base_lo_ok")
        lora_ps, route, lexp_ok, hw_ok = [sem(n) for n in ("lora_ps", "route", "lexp_ok", "hw_ok")]
        hwt_ps, hwt_hi_ok, hwt_lo_ok, y_ps, y_ok = [sem(n) for n in ("hwt_ps", "hwt_hi_ok", "hwt_lo_ok", "y_ps", "y_ok")]

        bb = sc
        ctx_raw = res[:, :, :].rearrange("p b d -> p (b d)").rearrange("p (h c n) -> p h c n", h=2, c=DC)
        xr_buf = [sc[:, :], pr[:, :], raw_o[:, 0:D], raw_o[:, D:2 * D]]
        base_hi = wqk_hi[:, :, :].rearrange("p h n -> p (h n)").rearrange("p (c n) -> p c n", c=DC)
        base_lo = wqk_lo[:, :, :].rearrange("p h n -> p (h n)").rearrange("p (c n) -> p c n", c=DC)
        LW = ER + E
        lora_hi = wv_hi[:, :, :].rearrange("p c n -> p (c n)")[:, 0:DC * LW].rearrange("p (c n) -> p c n", c=DC)
        lora_lo = wv_lo[:, :, :].rearrange("p c n -> p (c n)")[:, 0:DC * LW].rearrange("p (c n) -> p c n", c=DC)
        up_hi, up_lo = q_hi, q_lo
        hw = bm

        ROUTE_SHIFTED = 4
        ROUTE_STEPS = 24

        def wqk(w, hp, which, c):
            at = (which * DC + c) * P
            return w[:, hp, at:at + P]

        def three_passes(pe, dst, pairs, first=True, last=True):
            n, total = 0, 3 * len(pairs)
            for (l_hi, l_lo), (r_hi, r_lo) in pairs:
                for a, b in ((l_hi, r_hi), (l_hi, r_lo), (l_lo, r_hi)):
                    mm = pe.matmul(dst, a, b, start=first and n == 0, stop=last and n == total - 1)
                    n += 1
            return mm

        ctx_parts = [(0, slice(0, 2 * P), slice(0, 2 * P)), (0, slice(2 * P, W), slice(2 * P, W)),
                     (1, slice(0, W), slice(W, 2 * W))]

        def by_batch(bank):
            return bank[:, :].rearrange("p (b n) -> p b n", b=HALF)

        def batches(i):
            return (2 * i, 2 * i + 1)

        block = stack.enter_context(nc.Block())

        @block.sync
        def _(sp):
            sp.dma_start(acc[:, 0:HALF, :], x[:, 0:HALF, :]).then_inc(x_in[0], 16)
            sp.dma_start(raw_v[:, :], w_v[0, :, :]).then_inc(wv_in, 16)
            sp.dma_start(acc[:, HALF:B, :], x[:, HALF:B, :]).then_inc(x_in[1], 16)
            sp.dma_start(raw_qk[:, 0, :], w_qk[0, :, :]).then_inc(wqk_in[0], 16)
            sp.dma_start(raw_qk[:, 1, :], w_qk[1, :, :]).then_inc(wqk_in[1], 16)
            sp.dma_start(mask8[:, :, :], mask).then_inc(mask_in, 16)
            sp.dma_start(bias_sb[:, :, :], bias[0, :, :, :]).then_inc(bias_in, 16)
            sp.wait_ge(xr_used, B)
            sp.dma_start(raw_o[:, :], w_o[0, :, :]).then_inc(wo_in, 16)
            with sp.Fori(0, PAIRS - 1) as i:
                sp.wait_ge(wv_lo_ok, i + 1)
                sp.dma_start(raw_v[:, :], w_v[i + 1, :, :]).then_inc(wv_in, 16)
                for hp in range(2):
                    sp.wait_ge(wqk_lo_ok[hp], i + 1)
                    sp.dma_start(raw_qk[:, hp, :], w_qk[2 * i + (2 + hp), :, :]).then_inc(wqk_in[hp], 16)
                sp.wait_ge(wo_lo_ok, i + 1)
                sp.dma_start(raw_o[:, :], w_o[i + 1, :, :]).then_inc(wo_in, 16)
                sp.wait_ge(bm_ok, 4 * i + 4)
                sp.dma_start(bias_sb[:, :, :], bias[i + 1, :, :, :]).then_inc(bias_in, 16)
            sp.wait_ge(wv_lo_ok, PAIRS)
            sp.dma_start(raw_v[:, 0:DC * LW], w_lora).then_inc(lora_in, 16)
            sp.wait_ge(wqk_lo_ok[0], PAIRS)
            sp.wait_ge(wqk_lo_ok[1], PAIRS)
            sp.dma_start(raw_qk[:, :, :].rearrange("p h n -> p (h n)"), w_base).then_inc(base_in, 16)
            sp.wait_ge(wo_lo_ok, PAIRS)
            sp.dma_start(raw_o[:, 0:D], w_up).then_inc(up_in, 16)
            sp.wait_ge(exp_ok, STEPS)
            sp.dma_start(bb[:, :], b_base).then_inc(bb_in, 16)
            for t in range(B):
                sp.wait_ge(y_ok, t + 1)
                sp.dma_start(out[:, t, :], res[:, t, :]).then_inc(stored, 16)
            sp.wait_ge(stored, 16 * B)

        @block.gpsimd
        def _(pool):
            pool.memset(ident[:, :], 0.0).then_inc(ident_zero, 1)
            pool.wait_ge(ident_zero, 1)
            pool.affine_select(out=ident[:, :], in_=ident[:, :], compare_op=ALU.not_equal, fill=1.0,
                               base=0, pattern=[[-1, P]], channel_multiplier=1).then_inc(ident_ok, 1)
            for e in range(E):
                pool.memset(expert[:, e:e + 1], float(e)).then_inc(consts_ok, 1)
            pool.memset(half_pow[:, :, :], -0.5).then_inc(consts_ok, 1)
            pool.wait_ge(consts_ok, E + 1)
            steps = [0]

            def link(op):
                op.then_inc(pool_chain, 1)
                steps[0] += 1
                pool.wait_ge(pool_chain, steps[0])

            for h in range(2):
                own = slice(HALF * h, HALF * h + HALF)
                pool.wait_ge(mv_ok, HALF * h + HALF)
                mean, var = mv[:, own, 0], mv[:, own, 1]
                link(pool.tensor_scalar(scales[:, 0, own], var, EPS, 0.0, ALU.add, ALU.add))
                link(pool.tensor_scalar(scales[:, 1, own], scales[:, 0, own], EPS, 0.0, ALU.mult, ALU.add))
                link(pool.tensor_tensor(scales[:, 1, own], scales[:, 1, own], var, ALU.add))
                link(pool.tensor_tensor(scales[:, :, own], scales[:, :, own], half_pow[:, :, :], ALU.pow))
                link(pool.tensor_tensor(shift[:, own], mean, scales[:, 1, own], ALU.mult))
                pool.tensor_scalar(shift[:, own], shift[:, own], -1.0, 0.0, ALU.mult, ALU.add).then_inc(scales_ok, 1)
            pool.wait_ge(mask_in, 16)
            pool.tensor_scalar(mneg[:, :, :], mask8[:, :, :], -1.0, MASKED, ALU.add, ALU.mult).then_inc(mneg_ok, 1)
            pool.wait_ge(mneg_ok, 1)

            def start_sum(h):
                for t in range(HALF * h, HALF * h + HALF):
                    pool.wait_ge(ln_ok, t + 1)
                    pool.tensor_tensor(acc[:, t, :], res[:, t, :], acc[:, t, :], ALU.add).then_inc(acc_ok, 1)

            def mask_step(s, j, g):
                if j == 0:
                    pool.wait_ge(bias_in, 16 * g + 16)
                own = slice(HALF * (j // 2), HALF * (j // 2) + HALF)
                head_bias = bias_sb[:, j % 2:j % 2 + 1, :].to_broadcast([P, HALF, P])
                pool.tensor_tensor(bm[:, :, :], head_bias, mneg[:, own, :], ALU.add).then_inc(bm_ok, 1)

            def slot(s, j, g, following=True):
                if following:
                    pool.wait_ge(biased, s + 1)
                    mask_step(s + 1, (j + 1) % 4, g + 1 if j == 3 else g)
                pool.wait_ge(at_hi_ok, s + 1)
                pool.tensor_tensor(at_lo[:, j, :], at_full[:, :, :].rearrange("p b n -> p (b n)"),
                                   at_hi[:, j, :].bitcast(F32), ALU.subtract).then_inc(at_lo_ok, 1)

            mask_step(0, 0, 0)
            half, cols, own = ctx_parts[2]
            pool.wait_ge(ct_hi_ok, 3)
            pool.tensor_tensor(ct_lo[:, :, own], ctx_raw[:, half, :, cols], ct_hi[:, :, own].bitcast(F32),
                               ALU.subtract).then_inc(ct_last_ok, 1)
            pool.wait_ge(tanh_ok, 1)
            link(pool.tensor_scalar(gated[:, 0, :], scales[:, 0, :], tg[:, 0:1], -1.0, ALU.mult, ALU.mult))
            pool.tensor_tensor(gated[:, 1, :], mv[:, :, 0], gated[:, 0, :], ALU.mult).then_inc(gs_ok, 1)
            pool.wait_ge(gs_ok, 1)
            pool.tensor_scalar(gated[:, 0, :], gated[:, 0, :], -1.0, 0.0, ALU.mult, ALU.add).then_inc(gs_ok, 1)
            slot(0, 0, 0)
            start_sum(0)
            slot(1, 1, 0)
            start_sum(1)
            with pool.Fori(0, PAIRS - 1) as i:
                slot(4 * i + 2, 2, i)
                slot(4 * i + 3, 3, i)
                slot(4 * i + 4, 0, i + 1)
                slot(4 * i + 5, 1, i + 1)

            def base_weights_lo():
                pool.wait_ge(ffn_hi_ok, 2)
                pool.tensor_tensor(base_lo, raw_qk[:, :, :].rearrange("p h n -> p (h n)").rearrange("p (c n) -> p c n", c=DC),
                                   base_hi.bitcast(F32), ALU.subtract).then_inc(base_lo_ok, 1)

            def rstd1(h):
                own = slice(HALF * h, HALF * h + HALF)
                pool.wait_ge(mv1_ok, HALF * h + HALF)
                link(pool.tensor_scalar(scales[:, 0, own], mv[:, own, 1], EPS, 0.0, ALU.add, ALU.add))
                pool.tensor_tensor(scales[:, 0, own], scales[:, 0, own], half_pow[:, 0, :], ALU.pow).then_inc(rstd1_ok, 1)

            def add_bias(h):
                pool.wait_ge(x1n_ok, HALF * h + HALF)
                for t in range(HALF * h, HALF * h + HALF):
                    pool.tensor_tensor(acc[:, t, :], acc[:, t, :], bb[:, :], ALU.add).then_inc(x1b_ok, 1)

            slot(STEPS - 2, 2, PAIRS - 1)
            base_weights_lo()
            rstd1(0)
            slot(STEPS - 1, 3, PAIRS - 1, following=False)
            pool.wait_ge(bg_ok, 1)
            add_bias(0)
            rstd1(1)
            add_bias(1)

        @block.scalar
        def _(act):
            def load_ctx(n):
                half, cols, _ = ctx_parts[n]
                act.dma_start(ctx_raw[:, half, :, cols], ctx_t[half, :, :, cols]).then_inc(ctx_in[n], 16)

            load_ctx(0)
            load_ctx(1)
            act.dma_start(lnw[:, :], ln_w).then_inc(small_in, 16)
            act.dma_start(gate[:, :], gates).then_inc(small_in, 16)
            load_ctx(2)

            def ctx_part(n):
                half, cols, own = ctx_parts[n]
                act.wait_ge(ctx_in[n], 16)
                act.activation(ct_hi[:, :, own], ctx_raw[:, half, :, cols], ACT.Copy).then_inc(ct_hi_ok, 1)

            def split_wqk(hp, g):
                act.wait_ge(wqk_in[hp], 16 * g + 16)
                act.activation(wqk_hi[:, hp, :], raw_qk[:, hp, :], ACT.Copy).then_inc(wqk_hi_ok[hp], 1)

            def split_wv(g):
                act.wait_ge(wv_in, 16 * g + 16)
                act.activation(wv_hi[:, :, :], raw_v[:, :], ACT.Copy).then_inc(wv_hi_ok, 1)

            def split_wo(g):
                act.wait_ge(wo_in, 16 * g + 16)
                act.activation(wo_hi[:, :, :], raw_o[:, :], ACT.Copy).then_inc(wo_hi_ok, 1)

            def split_q(s):
                act.wait_ge(q_ps, s + 1)
                act.activation(q_hi[:, :], ps_q[:, :], ACT.Copy).then_inc(q_hi_ok, 1)

            def split_k(s):
                act.wait_ge(k_ps, s + 1)
                act.activation(k_hl[:, :, 0, :], by_batch(ps_k), ACT.Copy).then_inc(k_hi_ok, 1)

            def split_v(u, i, bank=ps_v):
                act.wait_ge(v_ps, u + 1)
                act.activation(v_hi[:, 2 * i:2 * i + 2, :], bank[:, :], ACT.Copy).then_inc(v_hi_ok, 1)

            def scale_tokens(h):
                act.wait_ge(scales_ok, h + 1)
                for t in range(HALF * h, HALF * h + HALF):
                    if h == 1:
                        act.wait_ge(xr_used, t - HALF + 1)
                    act.activation(xr_buf[t % HALF], acc[:, t, :], ACT.Identity, bias=shift[:, t:t + 1],
                                   scale=scales[:, 1, t:t + 1]).then_inc(xr_ok, 1)

            def token_hi(h):
                act.wait_ge(xr_used, HALF * h + HALF)
                for c in range(DC):
                    act.activation(xt_hi[:, c, W * h:W * h + W], ps_x[h][c][:, :], ACT.Copy,
                                   scale=lnw[:, c:c + 1]).then_inc(xt_hi_ok, 1)

            ctx_part(0)
            split_wv(0)
            ctx_part(1)
            scale_tokens(0)
            split_v(0, 0)
            split_wqk(0, 0)
            split_v(1, 1, bank=ps_w1)
            split_wqk(1, 0)
            act.wait_ge(small_in, 32)
            act.activation(tg[:, :], gate[:, :], ACT.Tanh).then_inc(tanh_ok, 1)
            token_hi(0)
            scale_tokens(1)
            split_k(0)
            split_q(0)
            ctx_part(2)
            token_hi(1)

            def slot(s, j, g, qk=True, v=True, start=False, before_attention=None):
                if j == 2 and v:
                    act.wait_ge(v_ps, s + 2)
                    split_wv(g + 1)
                if j == 2 and not v:
                    act.wait_ge(s_ps, s + 1)
                    split_wo(g)
                act.wait_ge(nmax_ok, s + 1)
                for k in range(HALF):
                    own = slice(P * k, P * k + P)
                    last = act.activation(pr[:, own], sc[:, own], ACT.Exp, bias=nmax[:, k:k + 1], accum_out=sums[:, k:k + 1])
                last.then_inc(exp_ok, 1)
                if qk:
                    split_q(s + 1)
                if j == 2 and v:
                    split_wo(g)
                if qk:
                    split_k(s + 1)
                act.wait_ge(t_ps, s + 1)
                act.activation(pt_hl[:, :, 0, :], by_batch(ps_t), ACT.Copy).then_inc(pt_hi_ok, 1)
                if j >= 2 and v:
                    split_wqk(j - 2, g + 1)
                if v and not start:
                    split_v(s + 2, (j + 2) % 4)
                if before_attention:
                    before_attention()
                act.wait_ge(a_ps, s + 1)
                act.activation(at_part[:, :, :], ps_w[:, :, 1, :], ACT.Copy).then_inc(at_part_ok, 1)
                act.wait_ge(at_full_ok, s + 1)
                act.activation(at_hi[:, j, :], at_full[:, :, :], ACT.Copy).then_inc(at_hi_ok, 1)
                if v and start:
                    split_v(s + 2, (j + 2) % 4)

            def gated_layernorm(some_batches):
                for t in some_batches:
                    act.activation(res[:, t, :], acc[:, t, :], ACT.Identity, bias=gated[:, 1, t:t + 1],
                                   scale=gated[:, 0, t:t + 1]).then_inc(ln_ok, 1)

            slot(0, 0, 0, start=True)
            act.wait_ge(gs_ok, 2)
            act.wait_ge(ct_lo_ok, 2)
            act.wait_ge(ct_last_ok, 1)
            gated_layernorm(range(0, 5))
            slot(1, 1, 0, start=True)
            gated_layernorm(range(5, B))
            with act.Fori(0, PAIRS - 1) as i:
                slot(4 * i + 2, 2, i)
                slot(4 * i + 3, 3, i)
                slot(4 * i + 4, 0, i + 1)
                slot(4 * i + 5, 1, i + 1)
            act.wait_ge(lora_in, 16)
            act.activation(lora_hi, raw_v[:, 0:DC * LW], ACT.Copy).then_inc(ffn_hi_ok, 1)

            def base_weights_hi():
                act.wait_ge(base_in, 16)
                act.activation(base_hi, raw_qk[:, :, :].rearrange("p h n -> p (h n)"), ACT.Copy).then_inc(ffn_hi_ok, 1)

            slot(STEPS - 2, 2, PAIRS - 1, v=False, before_attention=base_weights_hi)
            slot(STEPS - 1, 3, PAIRS - 1, qk=False, v=False)
            act.wait_ge(up_in, 16)
            act.activation(up_hi[:, :], raw_o[:, 0:D], ACT.Copy).then_inc(ffn_hi_ok, 1)

            def x1_hi(h):
                for t in range(HALF * h, HALF * h + HALF):
                    act.wait_ge(x1t_ps, t + 1)
                    act.activation(xt_hi[:, :, P * t:P * t + P], ps_x1[t][:, :], ACT.Copy).then_inc(x1t_hi_ok, 1)

            def router_exp(h):
                act.wait_ge(route, ROUTE_STEPS * h + ROUTE_SHIFTED)
                act.activation(lg[:, :, :], lg[:, :, :], ACT.Exp).then_inc(lexp_ok, 1)

            def hwt_hi(h):
                act.wait_ge(hwt_ps, h + 1)
                act.activation(pt_hl[:, :, 0, :], by_batch(ps_t), ACT.Copy).then_inc(hwt_hi_ok, 1)

            x1_hi(0)
            router_exp(0)
            hwt_hi(0)
            x1_hi(1)
            router_exp(1)
            hwt_hi(1)

        @block.vector
        def _(ve):
            def lo(dst, src, hi):
                return ve.tensor_tensor(dst, src, hi.bitcast(F32), ALU.subtract)

            def moments(batch_range, bn_sem, mv_sem):
                for t in batch_range:
                    ve.bn_stats(stats[:, t, :], acc[:, t, :]).then_inc(bn_sem, 1)
                for t in batch_range:
                    ve.wait_ge(bn_sem, t + 1)
                    ve.bn_aggr(mv[:, t, :], stats[:, t, :]).then_inc(mv_sem, 1)

            def ctx_part(n):
                half, cols, own = ctx_parts[n]
                ve.wait_ge(ct_hi_ok, n + 1)
                lo(ct_lo[:, :, own], ctx_raw[:, half, :, cols], ct_hi[:, :, own]).then_inc(ct_lo_ok, 1)

            def split_wqk(hp, g):
                ve.wait_ge(wqk_hi_ok[hp], g + 1)
                lo(wqk_lo[:, hp, :], raw_qk[:, hp, :], wqk_hi[:, hp, :]).then_inc(wqk_lo_ok[hp], 1)

            def split_wv(g):
                ve.wait_ge(wv_hi_ok, g + 1)
                lo(wv_lo[:, :, :], raw_v[:, :].rearrange("p (c n) -> p c n", c=DC), wv_hi[:, :, :]).then_inc(wv_lo_ok, 1)

            def split_wo(g):
                ve.wait_ge(wo_hi_ok, g + 1)
                lo(wo_lo[:, :, :], raw_o[:, :].rearrange("p (c n) -> p c n", c=2), wo_hi[:, :, :]).then_inc(wo_lo_ok, 1)

            def split_q(s):
                ve.wait_ge(q_hi_ok, s + 1)
                lo(q_lo[:, :], ps_q[:, :], q_hi[:, :]).then_inc(q_lo_ok, 1)

            def split_k(s):
                ve.wait_ge(k_hi_ok, s + 1)
                lo(k_hl[:, :, 1, :], by_batch(ps_k), k_hl[:, :, 0, :]).then_inc(k_lo_ok, 1)

            def split_v(u, i, bank=ps_v):
                ve.wait_ge(v_hi_ok, u + 1)
                own = slice(2 * i, 2 * i + 2)
                lo(v_lo[:, own, :], bank[:, :].rearrange("p (b n) -> p b n", b=2), v_hi[:, own, :]).then_inc(v_lo_ok, 1)

            def token_lo(h, chunks):
                for c in chunks:
                    ve.wait_ge(xt_hi_ok, DC * h + c + 1)
                    own = slice(W * h, W * h + W)
                    ve.scalar_tensor_tensor(xt_lo[:, c, own], ps_x[h][c][:, :], lnw[:, c:c + 1],
                                            xt_hi[:, c, own].bitcast(F32), ALU.mult, ALU.subtract).then_inc(xt_lo_ok, 1)

            def accumulate(w, i):
                for n, t in enumerate(batches(i)):
                    ve.wait_ge(o_ps, 2 * w + (n + 1))
                    ve.scalar_tensor_tensor(acc[:, t, :], ps_o[n][:, :], tg[:, 0:1], acc[:, t, :],
                                            ALU.mult, ALU.add).then_inc(acc_ok, 1)

            ve.wait_ge(x_in[0], 16)
            moments(range(0, HALF), bn_ok, mv_ok)
            ctx_part(0)
            split_wv(0)
            ctx_part(1)
            ve.wait_ge(x_in[1], 16)
            moments(range(HALF, B), bn_ok, mv_ok)
            split_v(0, 0)
            split_wqk(0, 0)
            split_v(1, 1, bank=ps_w1)
            split_wqk(1, 0)
            ve.wait_ge(small_in, 32)
            token_lo(0, range(DC))
            ve.wait_ge(mask_in, 16)
            ve.tensor_reduce(allowed[:, :], mask8[:, :, :], AX.X, ALU.max).then_inc(allowed_ok, 1)
            split_k(0)
            split_q(0)
            ve.wait_ge(allowed_ok, 1)

            def slot(s, j, g, qk=True, v=True, o=True, start=False, while_exp=None, while_pt=None, after_pt=None):
                ve.wait_ge(s_ps, s + 1)
                ve.wait_ge(bm_ok, s + 1)
                ve.tensor_tensor(by_batch(sc), ps_w[:, :, 1, :], bm[:, :, :], ALU.add).then_inc(biased, 1)
                ve.wait_ge(biased, s + 1)
                ve.tensor_tensor(by_batch(sc), ps_w[:, :, 0, :], by_batch(sc), ALU.add).then_inc(scored, 1)
                ve.wait_ge(scored, s + 1)
                ve.tensor_reduce(nmax[:, :], sc[:, :].rearrange("p (b k) -> p b k", b=HALF), AX.X, ALU.max,
                                 negate=True).then_inc(nmax_ok, 1)
                if j == 2 and v:
                    split_wv(g + 1)
                if j == 2 and not v:
                    split_wo(g)
                if while_exp:
                    while_exp()
                ve.wait_ge(exp_ok, s + 1)
                ve.reciprocal(rinv[:, :], sums[:, :]).then_inc(inv_ok, 1)
                ve.wait_ge(inv_ok, s + 1)
                for k in range(HALF):
                    own = slice(P * k, P * k + P)
                    t = HALF * (j // 2) + k
                    ve.tensor_scalar(pr[:, own], pr[:, own], rinv[:, k:k + 1], allowed[:, t:t + 1],
                                     ALU.mult, ALU.mult).then_inc(pr_ok, 1)
                if qk:
                    split_q(s + 1)
                if j == 2 and v:
                    split_wo(g)
                if qk:
                    split_k(s + 1)
                if while_pt:
                    while_pt()
                ve.wait_ge(pt_hi_ok, s + 1)
                lo(pt_hl[:, :, 1, :], by_batch(ps_t), pt_hl[:, :, 0, :]).then_inc(pt_lo_ok, 1)
                if after_pt:
                    after_pt()
                if j >= 2 and v:
                    split_wqk(j - 2, g + 1)
                if v and not start:
                    split_v(s + 2, (j + 2) % 4)
                ve.wait_ge(at_part_ok, s + 1)
                ve.tensor_tensor(at_full[:, :, :], ps_w[:, :, 0, :], at_part[:, :, :], ALU.add).then_inc(at_full_ok, 1)
                if v and start:
                    split_v(s + 2, (j + 2) % 4)
                if o:
                    accumulate(s - 2, (j + 2) % 4)

            slot(0, 0, 0, o=False, start=True, while_exp=lambda: token_lo(1, (0, 1)),
                 after_pt=lambda: token_lo(1, (2, 3)))
            slot(1, 1, 0, o=False, start=True)
            ve.wait_ge(tanh_ok, 1)
            with ve.Fori(0, PAIRS - 1) as i:
                slot(4 * i + 2, 2, i)
                slot(4 * i + 3, 3, i)
                slot(4 * i + 4, 0, i + 1)
                slot(4 * i + 5, 1, i + 1)

            def center1(some_batches):
                for t in some_batches:
                    ve.tensor_scalar(res[:, t, :], acc[:, t, :], mv[:, t, 0:1], scales[:, 0, t:t + 1],
                                     ALU.subtract, ALU.mult).then_inc(x1n_ok, 1)

            def accumulate_60():
                accumulate(STEPS - 4, 0)

            def accumulate_61():
                accumulate(STEPS - 3, 1)

            def moments_61():
                ve.wait_ge(acc_ok, B + 2 * (STEPS - 2))
                moments(range(2, HALF), bn1_ok, mv1_ok)

            def center_01():
                ve.wait_ge(rstd1_ok, 1)
                center1((0, 1))

            slot(STEPS - 2, 2, PAIRS - 1, v=False, o=False, after_pt=accumulate_60)
            ve.wait_ge(acc_ok, B + 2 * (STEPS - 3))
            moments(range(0, 2), bn1_ok, mv1_ok)
            slot(STEPS - 1, 3, PAIRS - 1, qk=False, v=False, o=False, while_exp=accumulate_61, while_pt=moments_61,
                 after_pt=center_01)

            def x1_lo(tokens_of):
                for t in tokens_of:
                    ve.wait_ge(x1t_hi_ok, t + 1)
                    own = slice(P * t, P * t + P)
                    lo(xt_lo[:, :, own], ps_x1[t][:, :].rearrange("p (c n) -> p c n", c=DC),
                       xt_hi[:, :, own]).then_inc(x1t_lo_ok, 1)

            steps = [0]

            def link(op, wait=True):
                op.then_inc(route, 1)
                steps[0] += 1
                if wait:
                    ve.wait_ge(route, steps[0])

            def spread(ap, n):
                return ap.unsqueeze(2).to_broadcast([P, HALF, n])

            def routing(h):
                for n in range(2):
                    ve.wait_ge(lora_ps, 2 * h + n + 1)
                    logits = ps_lora[n][:, 0:2 * LW].rearrange("p (b n) -> p b n", b=2)[:, :, ER:LW]
                    link(ve.tensor_copy(lg[:, 2 * n:2 * n + 2, :], logits), wait=n == 1)
                link(ve.tensor_reduce(lmax[:, :], lg[:, :, :], AX.X, ALU.max))
                link(ve.tensor_tensor(lg[:, :, :], lg[:, :, :], spread(lmax[:, :], E), ALU.subtract))
                assert steps[0] == ROUTE_STEPS * h + ROUTE_SHIFTED
                ve.wait_ge(lexp_ok, h + 1)
                link(ve.tensor_reduce(lsum[:, :], lg[:, :, :], AX.X, ALU.add))
                link(ve.reciprocal(linv[:, :], lsum[:, :]))
                link(ve.tensor_tensor(lg[:, :, :], lg[:, :, :], spread(linv[:, :], E), ALU.mult))
                for k in range(HALF):
                    link(ve.max(top[:, k, :], lg[:, k, :]), wait=k == HALF - 1)
                for k in range(HALF):
                    link(ve.max_index(top_i[:, k, :], top[:, k, :], lg[:, k, :]), wait=k == HALF - 1)
                link(ve.tensor_copy(top_f[:, :, :], top_i[:, :, 0:2]), wait=False)
                link(ve.tensor_tensor(lsum[:, :], top[:, :, 0], top[:, :, 1], ALU.add))
                link(ve.reciprocal(linv[:, :], lsum[:, :]))
                link(ve.scalar_tensor_tensor(tw[:, :, :], top[:, :, 0:2], SCALING, spread(linv[:, :], 2), ALU.mult, ALU.mult))
                numbers = expert[:, :].unsqueeze(1).to_broadcast([P, HALF, E])
                for n in range(2):
                    link(ve.tensor_tensor(hot[:, n, :, :], numbers, spread(top_f[:, :, n], E), ALU.is_equal), wait=n == 1)
                for n in range(2):
                    link(ve.tensor_tensor(hot[:, n, :, :], hot[:, n, :, :], spread(tw[:, :, n], E), ALU.mult), wait=n == 1)
                link(ve.tensor_tensor(comb[:, :, :], hot[:, 0, :, :], hot[:, 1, :, :], ALU.add))
                assert steps[0] == ROUTE_STEPS * (h + 1)
                if h == 1:
                    ve.wait_ge(hwt_ps, 1)
                for n in range(2):
                    hidden = ps_lora[n][:, 0:2 * LW].rearrange("p (b n) -> p b n", b=2)[:, :, 0:ER]
                    weight = comb[:, 2 * n:2 * n + 2, :].unsqueeze(3).to_broadcast([P, 2, E, R])
                    ve.tensor_tensor(hw[:, 2 * n:2 * n + 2, :].rearrange("p b (e r) -> p b e r", e=E),
                                     hidden.rearrange("p b (e r) -> p b e r", e=E), weight, ALU.mult).then_inc(hw_ok, 1)

            def hwt_lo(h):
                ve.wait_ge(hwt_hi_ok, h + 1)
                lo(pt_hl[:, :, 1, :], by_batch(ps_t), pt_hl[:, :, 0, :]).then_inc(hwt_lo_ok, 1)

            def finish(h):
                for t in range(HALF * h, HALF * h + HALF):
                    ve.wait_ge(y_ps, t + 1)
                    ve.wait_ge(x1b_ok, t + 1)
                    ve.scalar_tensor_tensor(res[:, t, :], ps_base[t % 4][:, :], tg[:, 1:2], acc[:, t, :],
                                            ALU.mult, ALU.add).then_inc(y_ok, 1)

            center1((2, 3))
            ve.wait_ge(ffn_hi_ok, 1)
            lo(lora_lo, raw_v[:, 0:DC * LW].rearrange("p (c n) -> p c n", c=DC), lora_hi).then_inc(ffn_lo_ok, 1)
            ve.wait_ge(bb_in, 16)
            ve.tensor_scalar(bb[:, :], bb[:, :], tg[:, 1:2], None, ALU.mult).then_inc(bg_ok, 1)
            x1_lo((0, 1, 2))
            for n in range(HALF):
                ve.wait_ge(last_ps, n + 1)
                ve.scalar_tensor_tensor(acc[:, HALF + n, :], ps_last[n][:, :], tg[:, 0:1], acc[:, HALF + n, :],
                                        ALU.mult, ALU.add).then_inc(acc_ok, 1)
            x1_lo((3,))
            ve.wait_ge(ffn_hi_ok, 3)
            lo(up_lo[:, :], raw_o[:, 0:D], up_hi[:, :]).then_inc(ffn_lo_ok, 1)
            ve.wait_ge(acc_ok, B + 2 * STEPS)
            moments(range(HALF, B), bn1_ok, mv1_ok)
            routing(0)
            ve.wait_ge(rstd1_ok, 2)
            center1((4, 5, 6, 7))
            hwt_lo(0)
            x1_lo((4, 5, 6))
            finish(0)
            x1_lo((7,))
            routing(1)
            hwt_lo(1)
            finish(1)

        @block.tensor
        def _(pe):
            def two_loads(pe, k, a_hi, a_lo, b_hl):
                pe.matmul(ps_w[:, k, :, :], a_hi, b_hl[:, k, :, :], start=True, stop=False)
                return pe.matmul(ps_w[:, k, 0, :], a_lo, b_hl[:, k, 0, :], start=False, stop=True)

            def project(dst, hp, which, token_hi, token_lo, half):
                own = slice(W * half, W * half + W)
                return three_passes(pe, dst, [((wqk(wqk_hi, hp, which, c), wqk(wqk_lo, hp, which, c)),
                                               (token_hi[:, c, own], token_lo[:, c, own])) for c in range(DC)])

            def queries(j):
                project(ps_q[:, :], j % 2, 0, xt_hi, xt_lo, j // 2).then_inc(q_ps, 1)

            def keys(j):
                project(ps_k[:, :], j % 2, 1, ct_hi, ct_lo, j // 2).then_inc(k_ps, 1)

            def values(i, which=(0, 1), bank=ps_v):
                for n in which:
                    t = batches(i)[n]
                    own = slice(P * t, P * t + P)
                    last = three_passes(pe, bank[:, 2 * P * n:2 * P * n + 2 * P],
                                        [((ct_hi[:, c, own], ct_lo[:, c, own]), (wv_hi[:, c, :], wv_lo[:, c, :]))
                                         for c in range(DC)])
                if n == 1:
                    last.then_inc(v_ps, 1)

            def output(i, which=(0, 1)):
                for n in which:
                    t = batches(i)[n]
                    own = slice(P * (t % HALF), P * (t % HALF) + P)
                    first = 2 * (t // HALF)
                    three_passes(pe, ps_o[n][:, :],
                                 [((at_hi[:, first + hp, own], at_lo[:, first + hp, own]),
                                   (wo_hi[:, hp, :], wo_lo[:, hp, :])) for hp in range(2)]).then_inc(o_ps, 1)

            def first_transposes(h):
                for t in range(HALF * h, HALF * h + HALF):
                    pe.wait_ge(xr_ok, t + 1)
                    for c in range(DC):
                        last = pe.transpose(ps_x[h][c][:, P * (t % HALF):P * (t % HALF) + P],
                                            xr_buf[t % HALF][:, P * c:P * c + P], ident[:, :])
                    last.then_inc(xr_used, 1)

            pe.wait_ge(ident_ok, 1)
            for _ in range(WARM_UP):
                pe.transpose(ps_w1[:, 0:P], ident[:, :], ident[:, :])
            pe.wait_ge(ct_lo_ok, 1)
            pe.wait_ge(wv_lo_ok, 1)
            values(0)
            pe.wait_ge(ct_lo_ok, 2)
            values(1, bank=ps_w1)
            first_transposes(0)
            pe.wait_ge(wqk_lo_ok[0], 1)
            keys(0)
            pe.wait_ge(xt_lo_ok, DC)
            queries(0)
            pe.wait_ge(v_lo_ok, 2)
            first_transposes(1)

            def slot(s, j, g, qk=True, v=True, o=True, start=False, first=False, before_transposes=None,
                     before_attention=None):
                nxt, ahead = (j + 1) % 4, (j + 2) % 4
                pe.wait_ge(q_lo_ok, s + 1)
                pe.wait_ge(k_lo_ok, s + 1)
                if not first:
                    pe.wait_ge(at_full_ok, s)
                for k in range(HALF):
                    own = slice(P * k, P * k + P)
                    last = two_loads(pe, k, q_hi[:, own], q_lo[:, own], k_hl)
                last.then_inc(s_ps, 1)
                if qk:
                    if nxt < 2:
                        pe.wait_ge(wqk_lo_ok[nxt], (g + 1 if j == 3 else g) + 1)
                    if start and j == 1:
                        pe.wait_ge(xt_lo_ok, 2 * DC)
                    queries(nxt)
                    keys(nxt)
                if start and j == 0:
                    pe.wait_ge(xt_lo_ok, DC + 2)
                    pe.wait_ge(ct_last_ok, 1)
                if before_transposes:
                    before_transposes()
                for k in range(HALF):
                    own = slice(P * k, P * k + P)
                    pe.wait_ge(pr_ok, HALF * s + (k + 1))
                    last = pe.transpose(ps_t[:, own], pr[:, own], ident[:, :])
                last.then_inc(t_ps, 1)
                if v or j == 2:
                    pe.wait_ge(v_lo_ok, s + 2)
                if v:
                    if ahead == 0:
                        pe.wait_ge(wv_lo_ok, g + 2)
                    values(ahead, (0,) if start else (0, 1))
                if before_attention:
                    before_attention()
                pe.wait_ge(pt_lo_ok, s + 1)
                if not first:
                    pe.wait_ge(at_lo_ok, s)
                for k in range(HALF):
                    t, hp = HALF * (j // 2) + k, j % 2
                    head = slice(P * hp, P * hp + P)
                    last = two_loads(pe, k, v_hi[:, t, head], v_lo[:, t, head], pt_hl)
                last.then_inc(a_ps, 1)
                if v and start:
                    values(ahead, (1,))
                if o:
                    if ahead == 0:
                        pe.wait_ge(wo_lo_ok, g + 1)
                    pe.wait_ge(acc_ok, B + 2 * s - 4)
                    output(ahead)

            slot(0, 0, 0, o=False, start=True, first=True)
            slot(1, 1, 0, o=False, start=True)
            with pe.Fori(0, PAIRS - 1) as i:
                slot(4 * i + 2, 2, i)
                slot(4 * i + 3, 3, i)
                slot(4 * i + 4, 0, i + 1)
                slot(4 * i + 5, 1, i + 1)

            def output_60():
                pe.wait_ge(wo_lo_ok, PAIRS)
                pe.wait_ge(at_lo_ok, STEPS - 2)
                pe.wait_ge(acc_ok, B + 2 * (STEPS - 4))
                output(0)

            def last_output(n, heads):
                own = slice(P * n, P * n + P)
                mm = three_passes(pe, ps_last[n][:, :],
                                  [((at_hi[:, 2 + hp, own], at_lo[:, 2 + hp, own]), (wo_hi[:, hp, :], wo_lo[:, hp, :]))
                                   for hp in heads], first=0 in heads, last=1 in heads)
                if 1 in heads:
                    mm.then_inc(last_ps, 1)

            def before_last_transposes():
                output(1, (1,))
                pe.wait_ge(at_lo_ok, STEPS - 1)
                last_output(0, (0,))
                last_output(1, (0,))
                last_output(2, (0,))

            def before_last_attention():
                last_output(3, (0,))

            slot(STEPS - 2, 2, PAIRS - 1, v=False, o=False, before_attention=output_60)
            pe.wait_ge(acc_ok, B + 2 * (STEPS - 3))
            output(1, (0,))
            slot(STEPS - 1, 3, PAIRS - 1, qk=False, v=False, o=False, before_transposes=before_last_transposes,
                 before_attention=before_last_attention)

            def x1_transposes(t):
                pe.wait_ge(x1n_ok, t + 1)
                for c in range(DC):
                    last = pe.transpose(ps_x1[t][:, P * c:P * c + P], res[:, t, P * c:P * c + P], ident[:, :])
                last.then_inc(x1t_ps, 1)

            def tokens(t):
                own = slice(P * t, P * t + P)
                return [(xt_hi[:, c, own], xt_lo[:, c, own]) for c in range(DC)]

            def lora(t):
                n = t % HALF
                pe.wait_ge(x1t_lo_ok, 6 if t == 4 else t + 1)
                mm = three_passes(pe, ps_lora[n // 2][:, LW * (n % 2):LW * (n % 2) + LW],
                                  [(tok, (lora_hi[:, c, :], lora_lo[:, c, :])) for c, tok in enumerate(tokens(t))])
                if n % 2:
                    mm.then_inc(lora_ps, 1)

            def base(t):
                if t >= HALF:
                    pe.wait_ge(y_ok, t - 3)
                three_passes(pe, ps_base[t % 4][:, :],
                             [(tok, (base_hi[:, c, :], base_lo[:, c, :])) for c, tok in enumerate(tokens(t))],
                             last=False)

            def hw_transposes(h):
                pe.wait_ge(hw_ok, 2 * h + 2)
                for k in range(HALF):
                    last = pe.transpose(ps_t[:, P * k:P * k + P], hw[:, k, :], ident[:, :])
                last.then_inc(hwt_ps, 1)

            def up(t):
                pe.wait_ge(hwt_lo_ok, t // HALF + 1)
                three_passes(pe, ps_base[t % 4][:, :], [((pt_hl[:, t % HALF, 0, :], pt_hl[:, t % HALF, 1, :]),
                                                         (up_hi[:, :], up_lo[:, :]))],
                             first=False).then_inc(y_ps, 1)

            x1_transposes(0)
            x1_transposes(1)
            pe.wait_ge(at_full_ok, STEPS)
            x1_transposes(2)
            pe.wait_ge(at_lo_ok, STEPS)
            for n in range(HALF):
                last_output(n, (1,))
            pe.wait_ge(x1t_lo_ok, 1)
            x1_transposes(3)
            pe.wait_ge(ffn_lo_ok, 1)
            for t in range(HALF):
                lora(t)
            pe.wait_ge(base_lo_ok, 1)
            pe.wait_ge(acc_ok, B + 2 * STEPS)
            base(0)
            base(1)
            base(2)
            hw_transposes(0)
            for t in (4, 5, 6):
                x1_transposes(t)
            base(3)
            pe.wait_ge(ffn_lo_ok, 2)
            for t in range(HALF):
                up(t)
            x1_transposes(7)
            for t in range(HALF, B):
                lora(t)
            base(4)
            base(5)
            hw_transposes(1)
            base(6)
            up(4)
            up(5)
            base(7)
            up(6)
            up(7)

def _layouts(x, ctx_4096, mask_BxSxS2_bk0, g_xattn, g_ffn, L0_xattn_position_bias, L0_xattn_ln_weight,
             L0_xattn_w_q, L0_xattn_w_k, L0_xattn_w_v, L0_xattn_w_out, L0_ffn_W_base, L0_ffn_b_base,
             L0_ffn_W_router, L0_ffn_A, L0_ffn_B):
    import numpy as np
    a = np.asarray

    def chunks(w, n):
        w = a(w)
        return w.reshape(-1, n, DC, P).transpose(0, 3, 2, 1).reshape(-1, P, DC * n)

    lora_in = np.concatenate([a(L0_ffn_A).reshape(ER, D), a(L0_ffn_W_router)], axis=0)
    return {
        "x": a(x).transpose(1, 0, 2),
        "ctx_t": a(ctx_4096).reshape(2, W, DC, P).transpose(0, 3, 2, 1),
        "mask": a(mask_BxSxS2_bk0).transpose(1, 0, 2),
        "gates": np.broadcast_to(np.concatenate([a(g_xattn), a(g_ffn)]), (P, 2)),
        "bias": a(L0_xattn_position_bias).reshape(PAIRS, 2, P, P).transpose(0, 2, 1, 3),
        "ln_w": a(L0_xattn_ln_weight).reshape(DC, P).T,
        "w_qk": np.concatenate([chunks(L0_xattn_w_q, P), chunks(L0_xattn_w_k, P)], axis=2),
        "w_v": chunks(L0_xattn_w_v, 2 * P),
        "w_o": a(L0_xattn_w_out).reshape(D, PAIRS, 2, P).transpose(1, 3, 2, 0).reshape(PAIRS, P, 2 * D),
        "w_base": chunks(L0_ffn_W_base, D)[0],
        "w_lora": chunks(lora_in, ER + E)[0],
        "w_up": a(L0_ffn_B).transpose(0, 2, 1).reshape(ER, D),
        "b_base": np.broadcast_to(a(L0_ffn_b_base), (P, D)),
    }


def kernel(**inputs):
    import numpy as np
    import concourse.bacc as bacc
    from concourse.bass_utils import run_bass_kernel_spmd

    nc = bacc.Bacc("TRN2", target_bir_lowering=False, num_devices=1)
    arrays, args = {}, {}
    for name, array in _layouts(**inputs).items():
        array = np.ascontiguousarray(array)
        arrays[f"in_{name}"] = array
        args[name] = nc.dram_tensor(f"in_{name}", array.shape, mybir.dt.from_np(array.dtype), kind="ExternalInput").ap()
    args["out"] = nc.dram_tensor("out_y", (P, B, D), F32, kind="ExternalOutput").ap()
    flamingo_block(nc, **args)
    result = run_bass_kernel_spmd(nc, [arrays], core_ids=[0])
    return np.ascontiguousarray(result.results[0]["out_y"].transpose(1, 0, 2))
```
